# Optimizing a Trainium2 kernel written in Bass

```python
import numpy as np
import jax
import jax.numpy as jnp

def _softmax(x, axis=-1):
    return jax.nn.softmax(x, axis=axis)

def _gelu(x):
    return jax.nn.gelu(x, approximate=True)

def _silu(x):
    return jax.nn.silu(x)

def _sigmoid(x):
    return jax.nn.sigmoid(x)

def _layernorm(x, axis=-1, eps=1e-05):
    m = jnp.mean(x, axis=axis, keepdims=True)
    v = jnp.var(x, axis=axis, keepdims=True)
    return (x - m) / jnp.sqrt(v + eps)

def _scatter_add(tgt, idx, src, axis=0):
    return tgt.at[idx].add(src)

def _segment_sum(src, seg, n):
    return jax.ops.segment_sum(src, seg, n)
kernel_name = 'mk_xattn_ffn_d1_seqx_r8_8e9638'

def setup_inputs(seed: int=0):
    np.random.seed(seed)
    _w = jnp.asarray

    def _rec_inputs():
        import jax
        import jax.numpy as jnp
        _rk = jax.random.key(seed)
        x = 7.22e-05 + 1 * jax.random.normal(jax.random.fold_in(_rk, 1), (128, 64, 128), jnp.float32)
        _lenS = 64 - jax.random.randint(jax.random.fold_in(_rk, 7), (128,), 0, max(1, 64 // 4) + 1, jnp.int32)
        _lenS2 = 64 - jax.random.randint(jax.random.fold_in(_rk, 8), (128,), 0, max(1, 64 // 4) + 1, jnp.int32)
        _ctx_1024P = jax.random.normal(jax.random.fold_in(_rk, 11), (128, 16, 128), jnp.float32)
        _ctx_1024c = jax.random.dirichlet(jax.random.fold_in(_rk, 511), 0.3 * jnp.ones((16,), jnp.float32), (128, 64))
        _ctx_1024t = jnp.einsum('bsk,bkd->bsd', _ctx_1024c, _ctx_1024P)
        _ctx_1024t = _ctx_1024t * jax.lax.rsqrt(jnp.mean(jnp.square(_ctx_1024t)) + 1e-12) * 0.953939
        ctx_1024 = 4.13588e-05 + 0.999923 * (_ctx_1024t + 0.3 * jax.random.normal(jax.random.fold_in(_rk, 611), (128, 64, 128), jnp.float32))
        return (x, ctx_1024)
    x, ctx_1024 = _rec_inputs()

    def _L0_xattn_setup():
        import jax, jax.numpy as jnp
        import numpy as np
        BETA = 128
        NUM_HEADS = 16
        NORM = (BETA // NUM_HEADS) ** (-0.5)
        key = jax.random.key(seed)
        ks = jax.random.split(key, 6)
        B, N = (4, 256)
        D_in_q = D_in_k = D_in_v = 128
        D_out_k = D_out_v = 128
        q = jax.random.normal(ks[0], (B, N, D_in_q), dtype=jnp.float32)
        k = jax.random.normal(ks[1], (B, N, D_in_k), dtype=jnp.float32)
        v = jax.random.normal(ks[2], (B, N, D_in_v), dtype=jnp.float32)
        Wq = jax.random.normal(ks[3], (D_out_k, D_in_q), dtype=jnp.float32) * D_in_q ** (-0.5)
        Wk = jax.random.normal(ks[4], (D_out_k, D_in_k), dtype=jnp.float32) * D_in_k ** (-0.5)
        Wv = jax.random.normal(ks[5], (D_out_v, D_in_v), dtype=jnp.float32) * D_in_v ** (-0.5)
        return {'q': q, 'k': k, 'v': v, 'Wq': Wq, 'Wk': Wk, 'Wv': Wv}
    _L0_xattn_all = _L0_xattn_setup()
    _L0_xattn_in = {k: v for k, v in _L0_xattn_all.items() if k in ('Wq', 'Wk', 'Wv')}
    del _L0_xattn_all

    def _L0_ffn_setup():
        import jax, jax.numpy as jnp
        import numpy as np
        B, S, D = (2, 512, 128)
        H = 512
        E = 8
        K = 4
        key = jax.random.key(seed)
        kx, kr, ku, kd = jax.random.split(key, 4)
        x = jax.random.normal(kx, (B, S, D), dtype=jnp.float32)
        router_w = jax.random.normal(kr, (D, E), dtype=jnp.float32) / np.sqrt(D)
        up_w = jax.random.normal(ku, (E, D, H), dtype=jnp.float32) / np.sqrt(D)
        down_w = jax.random.normal(kd, (E, H, D), dtype=jnp.float32) / np.sqrt(H)
        return {'x': x, 'router_w': router_w, 'up_w': up_w, 'down_w': down_w}
    _L0_ffn_all = _L0_ffn_setup()
    _L0_ffn_in = {k: v for k, v in _L0_ffn_all.items() if k in ('router_w', 'up_w', 'down_w')}
    del _L0_ffn_all
    return {'x': x, 'ctx_1024': ctx_1024, 'L0_xattn_Wq': _L0_xattn_in['Wq'], 'L0_xattn_Wk': _L0_xattn_in['Wk'], 'L0_xattn_Wv': _L0_xattn_in['Wv'], 'L0_ffn_router_w': _L0_ffn_in['router_w'], 'L0_ffn_up_w': _L0_ffn_in['up_w'], 'L0_ffn_down_w': _L0_ffn_in['down_w']}

def reference(x, ctx_1024, L0_xattn_Wq, L0_xattn_Wk, L0_xattn_Wv, L0_ffn_router_w, L0_ffn_up_w, L0_ffn_down_w):
    import jax
    import jax.numpy as jnp

    def _L0_xattn_ref(q, k, v, Wq, Wk, Wv):
        import jax, jax.numpy as jnp
        import numpy as np
        BETA = 128
        NUM_HEADS = 16
        NORM = (BETA // NUM_HEADS) ** (-0.5)
        qp = jax.nn.relu(jnp.einsum('bnd,od->bno', q, Wq))
        kp = jax.nn.relu(jnp.einsum('bnd,od->bno', k, Wk))
        vp = jax.nn.relu(jnp.einsum('bnd,od->bno', v, Wv))
        B, N, D = qp.shape
        dh = D // NUM_HEADS
        qh = qp.reshape(B, N, NUM_HEADS, dh)
        kh = kp.reshape(B, N, NUM_HEADS, dh)
        vh = vp.reshape(B, N, NUM_HEADS, vp.shape[-1] // NUM_HEADS)
        E = NORM * jnp.einsum('bqhd,bkhd->bhqk', qh, kh)
        A = jax.nn.softmax(E, axis=-1)
        out = jnp.einsum('bhqk,bkhd->bqhd', A, vh)
        return out.reshape(B, N, -1)

    def _L0_ffn_ref(x, router_w, up_w, down_w):
        import jax, jax.numpy as jnp
        import numpy as np
        B, S, D = (2, 512, 128)
        H = 512
        E = 8
        K = 4
        router_logits = jnp.einsum('bsd,de->bse', x, router_w)
        routing_weights = jax.nn.softmax(router_logits, axis=-1)
        topk_weights, topk_indices = jax.lax.top_k(routing_weights, K)
        topk_weights = topk_weights / jnp.sum(topk_weights, axis=-1, keepdims=True)
        h = jnp.einsum('bsd,edh->bseh', x, up_w)
        h = jax.nn.gelu(h)
        expert_outputs = jnp.einsum('bseh,ehd->bsed', h, down_w)
        gathered = jnp.take_along_axis(expert_outputs, topk_indices[:, :, :, None], axis=2)
        output = jnp.sum(topk_weights[:, :, :, None] * gathered, axis=2)
        return output
    x = x + _L0_xattn_ref(_layernorm(x, axis=-1), ctx_1024, ctx_1024, L0_xattn_Wq, L0_xattn_Wk, L0_xattn_Wv)
    x = x + _L0_ffn_ref(_layernorm(x, axis=-1), L0_ffn_router_w, L0_ffn_up_w, L0_ffn_down_w)
    return x

_drawn_inputs = setup_inputs


def setup_inputs(seed=0):
    import zlib

    import numpy as np

    out = dict(_drawn_inputs(seed))
    spreads = {}
    factors = {}
    for name, (base, spread) in spreads.items():
        noise = np.random.default_rng([zlib.crc32(name.encode()), seed]).standard_normal(out[name].shape)
        drawn = base * np.exp(spread * noise) if base else spread * noise
        out[name] = jnp.asarray(drawn.astype(out[name].dtype))
    for name, factor in factors.items():
        out[name] = (out[name] * factor).astype(out[name].dtype)
    return out
```

```python
from contextlib import ExitStack

import concourse.bass as bass
from concourse import mybir

F32 = mybir.dt.float32
F32R = mybir.dt.float32r
ALU = mybir.AluOpType
ACT = mybir.ActivationFunctionType
AX = mybir.AxisListType

P = 128
HEADS = 16
TOPK = 4
EPS = 1e-5
E_BASE = 2.718281828459045


def build(nc, x, ctx_in, wq, wk, wv, router_w, up_w, down_w, out):
    NSEQ, SEQ, D = x.shape
    _, _, HID = up_w.shape
    E = router_w.shape[1]
    DH = D // HEADS
    NORM = float(DH) ** -0.5
    PAIR = 2 * SEQ
    TOK = 512
    PAIRS = TOK // PAIR
    G = NSEQ * SEQ // TOK
    S = 2
    J = HEADS // S
    PARTS = 4
    T = HEADS // 2
    CH = HID // P
    U = E * CH
    HALF = PAIRS * SEQ
    LAG = 2
    NH = 4
    assert PAIR == P and D == P and S * 2 * PARTS * DH == P and G % 2 == 0

    x_v = x.rearrange("(g r b) s d -> g (b s) r d", r=PAIRS, b=2)
    c_v = ctx_in.rearrange("(g r b) s d -> g (b s) r d", r=PAIRS, b=2)
    o_v = out.rearrange("(g r b) s d -> g (b s) r d", r=PAIRS, b=2)

    with ExitStack() as stack:
        def sb(name, shape, dt=F32):
            return stack.enter_context(nc.sbuf_tensor(name, shape, dt))

        def ps(name, shape):
            return stack.enter_context(nc.psum_tensor(name, shape, F32))

        def sem(name):
            return stack.enter_context(nc.semaphore(name))

        up_hi = sb("up_hi", [P, E, HID], F32R)
        up_lo = sb("up_lo", [P, E, HID], F32R)
        dn_hi = sb("dn_hi", [P, E, CH, D], F32R)
        dn_lo = sb("dn_lo", [P, E, CH, D], F32R)
        w_raw = sb("w_raw", [P, 3, D])
        w_hi = sb("w_hi", [P, 3, D], F32R)
        w_lo = sb("w_lo", [P, 3, D], F32R)
        r_raw = sb("r_raw", [P, E])
        r_hi = sb("r_hi", [P, E], F32R)
        r_lo = sb("r_lo", [P, E], F32R)
        ident = sb("ident", [P, P])
        pick = sb("pick", [P, E, P], F32R)
        earlier = sb("earlier", [P, E, E])
        minus_half = sb("minus_half", [P, PAIRS])
        e_base = sb("e_base", [P, PAIRS * E])
        x_in = sb("x_in", [P, PAIRS, D])
        c_in = sb("c_in", [P, PAIRS, D])
        stats = sb("stats", [P, PAIRS, 6])
        mean_var = sb("mean_var", [P, PAIRS, 2])
        var_eps = sb("var_eps", [P, PAIRS])
        rstd = sb("rstd", [P, PAIRS])
        xn = sb("xn", [P, PAIRS, D])
        cT_hi = sb("cT_hi", [P, TOK], F32R)
        cT_lo = sb("cT_lo", [P, TOK], F32R)
        xT_hi = sb("xT_hi", [P, TOK], F32R)
        xT_lo = sb("xT_lo", [P, TOK], F32R)
        q_hi = sb("q_hi", [P, 2, SEQ, PAIRS], F32R)
        q_lo = sb("q_lo", [P, 2, SEQ, PAIRS], F32R)
        k_hi = sb("k_hi", [P, 2, PAIRS, SEQ], F32R)
        k_lo = sb("k_lo", [P, 2, PAIRS, SEQ], F32R)
        v_sb = sb("v_sb", [P, PAIRS, 2, DH * T])
        q_rows = sb("q_rows", [P, J, 2 * SEQ, PAIRS], F32R)
        k_rows = sb("k_rows", [P, J, PAIRS, SEQ], F32R)
        v_rows = sb("v_rows", [P, PAIRS, 2, 2, (DH + 1) * T])
        row_max = sb("row_max", [P, HEADS])
        probs = sb("probs", [P, PAIRS, HEADS, SEQ])
        probsT = sb("probsT", [P, T, P])
        inv_sum = sb("inv_sum", [P, HEADS])
        att = sb("att", [P, HEADS, DH])
        x1 = sb("x1", [P, 2, PAIRS, D])
        x2_hi = sb("x2_hi", [P, 2, TOK], F32R)
        x2_lo = sb("x2_lo", [P, 2, TOK], F32R)
        wT = sb("wT", [P, 2, TOK], F32R)
        logit_max = sb("logit_max", [P, PAIRS])
        logits = sb("logits", [P, PAIRS, E])
        expert_p = sb("expert_p", [P, PAIRS, E])
        above = sb("above", [P, PAIRS, E, E])
        same = sb("same", [P, PAIRS, E, E])
        rank = sb("rank", [P, PAIRS, E])
        w_sel = sb("w_sel", [P, PAIRS, E])
        w_sum = sb("w_sum", [P, PAIRS])
        w_inv = sb("w_inv", [P, PAIRS])
        w_norm = sb("w_norm", [P, PAIRS, E])
        w_round = sb("w_round", [P, PAIRS, E], F32R)
        w_split = sb("w_split", [P, PAIRS, 2, E])
        h_full = sb("h_full", [P, 2, TOK])
        h_hi = sb("h_hi", [P, NH, TOK], F32R)
        h_lo = sb("h_lo", [P, NH, TOK], F32R)
        wb = sb("wb", [P, 2, TOK])
        prod = sb("prod", [P, 2, TOK])
        acc = sb("acc", [P, 2, TOK])
        o_sb = sb("o_sb", [P, PAIRS, D])

        p_s = ps("p_s", [P, 2, 512])
        p_t = ps("p_t", [P, 512])
        p_m = ps("p_m", [P, 512])
        p_f = ps("p_f", [P, 512])
        p_u = ps("p_u", [P, 2, 512])
        p_y = ps("p_y", [P, 512])

        up_loaded = sem("up_loaded")
        dn_loaded = sem("dn_loaded")
        w_loaded = sem("w_loaded")
        x_loaded = sem("x_loaded")
        c_loaded = sem("c_loaded")
        q_placed = sem("q_placed")
        k_placed = sem("k_placed")
        v_placed = sem("v_placed")
        stored = sem("stored")
        pool_const = sem("pool_const")
        zeroed = sem("zeroed")
        w_turned = sem("w_turned")
        const_step = sem("const_step")
        w_step = sem("w_step")
        up_split = sem("up_split")
        dn_split = sem("dn_split")
        w_split_done = sem("w_split_done")
        pick_ready = sem("pick_ready")
        var_ready = sem("var_ready")
        rstd_ready = sem("rstd_ready")
        ln_step = sem("ln_step")
        xn_ready = sem("xn_ready")
        c_turned = sem("c_turned")
        x_turned = sem("x_turned")
        cT_hi_ready = sem("cT_hi_ready")
        cT_lo_ready = sem("cT_lo_ready")
        xT_hi_ready = sem("xT_hi_ready")
        xT_lo_ready = sem("xT_lo_ready")
        k_made = sem("k_made")
        v_made = sem("v_made")
        q_made = sem("q_made")
        k_hi_ready = sem("k_hi_ready")
        k_lo_ready = sem("k_lo_ready")
        v_ready = sem("v_ready")
        q_hi_ready = sem("q_hi_ready")
        q_lo_ready = sem("q_lo_ready")
        scores_ready = sem("scores_ready")
        max_ready = sem("max_ready")
        shifted = sem("shifted")
        exp_done = sem("exp_done")
        turned = sem("turned")
        pT_ready = sem("pT_ready")
        av_done = sem("av_done")
        sums_ready = sem("sums_ready")
        o_read = sem("o_read")
        x1_ready = sem("x1_ready")
        x2_turned = sem("x2_turned")
        x2_hi_ready = sem("x2_hi_ready")
        x2_lo_ready = sem("x2_lo_ready")
        logits_ready = sem("logits_ready")
        route_step = sem("route_step")
        logits_read = sem("logits_read")
        pool_route = sem("pool_route")
        rank_in = sem("rank_in")
        weights_ready = sem("weights_ready")
        wT_turned = sem("wT_turned")
        round_done = sem("round_done")
        compared = sem("compared")
        wT_ready = sem("wT_ready")
        wb_made = sem("wb_made")
        wb_ready = sem("wb_ready")
        up_done = sem("up_done")
        h_full_ready = sem("h_full_ready")
        h_hi_ready = sem("h_hi_ready")
        h_hi_dve = sem("h_hi_dve")
        h_lo_ready = sem("h_lo_ready")
        h_lo_pool = sem("h_lo_pool")
        down_done = sem("down_done")
        prod_ready = sem("prod_ready")
        acc_ready = sem("acc_ready")
        out_turned = sem("out_turned")
        out_ready = sem("out_ready")

        block = stack.enter_context(nc.Block())

        def f32(ap):
            return ap.bitcast(F32)

        def by_group(eng, attend, experts, drain):
            for slot in range(U):
                attend(0, 0, slot)
            for slot in range(U):
                experts(0, 0, slot)
                attend(1, 1, slot)
            with eng.Fori(0, G // 2 - 1) as i:
                for odd in (1, 0):
                    g = 2 * i + 2 - odd
                    for slot in range(U):
                        experts(g, odd, slot)
                        attend(g + 1, 1 - odd, slot)
            for slot in range(U):
                experts(G - 1, 1, slot)
            drain(G)

        @block.sync
        def _(sp):
            for i, w in enumerate((wk, wv, wq)):
                sp.dma_start(w_raw[:, i, :], w).then_inc(w_loaded, 16)
            sp.dma_start(r_raw[:], router_w).then_inc(w_loaded, 16)

            def attend(g, odd, slot):
                if slot == 0:
                    if not (isinstance(g, int) and g == 0):
                        sp.wait_ge(x1_ready, PAIRS * g)
                    sp.dma_start(c_in[:], c_v[g]).then_inc(c_loaded, 16)
                    sp.dma_start(x_in[:], x_v[g]).then_inc(x_loaded, 16)
                    if isinstance(g, int) and g == 0:
                        raw = probs[:].rearrange("p r h k -> p (r h k)")
                        sp.wait_ge(pick_ready, 1)
                        sp.dma_start(raw.rearrange("p (e h) -> p e h", e=E),
                                     up_w.rearrange("e d h -> d e h")).then_inc(up_loaded, 16)
                        sp.wait_ge(up_split, 2)
                        sp.dma_start(raw.rearrange("p (e c d) -> p e c d", e=E, c=CH),
                                     down_w.rearrange("e (c p) d -> p e c d", p=P)).then_inc(dn_loaded, 16)
                if slot == 6:
                    sp.wait_ge(k_hi_ready, g + 1)
                    sp.wait_ge(k_lo_ready, g + 1)
                    if isinstance(g, int) and g == 0:
                        sp.wait_ge(zeroed, 3)
                    for s in range(S):
                        for b in range(2):
                            for part in range(PARTS):
                                row = 2 * PARTS * DH * s + PARTS * DH * b + DH * part
                                src = (k_hi, k_lo)[part % 2]
                                sp.dma_start(f32(k_rows[row:row + DH, :, :, :]),
                                             f32(src[64 * s:64 * s + 64, b, :, :])).then_inc(k_placed, 16)
                    sp.wait_ge(v_ready, g + 1)
                    for hp in range(2):
                        for b in range(2):
                            sp.dma_start(v_rows[64 * hp:64 * hp + 64, :, b, hp, 0:DH * T],
                                         v_sb[64 * b:64 * b + 64, :, hp, :]).then_inc(v_placed, 16)
                if slot == 8:
                    sp.wait_ge(q_hi_ready, g + 1)
                    sp.wait_ge(q_lo_ready, g + 1)
                    for s in range(S):
                        for b in range(2):
                            for part in range(PARTS):
                                row = 2 * PARTS * DH * s + PARTS * DH * b + DH * part
                                src = (q_hi, q_lo)[part // 2]
                                sp.dma_start(f32(q_rows[row:row + DH, :, SEQ * b:SEQ * b + SEQ, :]),
                                             f32(src[64 * s:64 * s + 64, b, :, :])).then_inc(q_placed, 16)

            def store(g):
                sp.wait_ge(out_ready, g + 1)
                sp.dma_start(o_v[g], o_sb[:]).then_inc(stored, 16)

            def experts(g, odd, slot):
                if slot == 7 and not (isinstance(g, int) and g == 0):
                    store(g - 1)

            def drain(g):
                store(g - 1)
                sp.wait_ge(stored, 16 * G)

            by_group(sp, attend, experts, drain)

        @block.gpsimd
        def _(pool):
            sel = probs[:, 0, :, :].rearrange("p h k -> p (h k)").rearrange("p (e m) -> p e m", e=E)
            nc.gpsimd.memset(ident[:], 0.0).then_inc(pool_const, 1)
            nc.gpsimd.memset(earlier[:], 1.0).then_inc(pool_const, 1)
            nc.gpsimd.memset(sel, 0.0).then_inc(pool_const, 1)
            nc.gpsimd.memset(minus_half[:], -0.5)
            nc.gpsimd.memset(e_base[:], E_BASE).then_inc(pool_const, 1)
            pool.wait_ge(pool_const, 4)
            nc.gpsimd.affine_select(out=ident[:], in_=ident[:], compare_op=ALU.not_equal, fill=1.0, base=0,
                                    pattern=[[-1, P]], channel_multiplier=1).then_inc(pool_const, 1)
            nc.gpsimd.affine_select(out=earlier[:], in_=earlier[:], compare_op=ALU.is_gt, fill=0.0, base=0,
                                    pattern=[[1, E], [-1, E]], channel_multiplier=0).then_inc(pool_const, 1)
            nc.gpsimd.affine_select(out=sel, in_=sel, compare_op=ALU.not_equal, fill=1.0, base=0,
                                    pattern=[[-1, E], [0, P]], channel_multiplier=1).then_inc(pool_const, 1)
            pool.wait_ge(pool_const, 7)
            nc.gpsimd.affine_select(out=sel, in_=sel, compare_op=ALU.not_equal, fill=1.0, base=-E,
                                    pattern=[[-1, E], [0, P]], channel_multiplier=1).then_inc(pool_const, 1)

            def attend(g, odd, slot):
                if slot in (2, 25):
                    k = slot == 25
                    pool.wait_ge(var_ready, 2 * g + k + 1)
                    nc.gpsimd.tensor_tensor(rstd[:], var_eps[:], minus_half[:], ALU.pow).then_inc(rstd_ready, 1)
                if slot == 30:
                    pool.wait_ge(logits_read, g + 1)
                    nc.gpsimd.tensor_tensor(expert_p[:].rearrange("p r e -> p (r e)"), e_base[:],
                                            logits[:].rearrange("p r e -> p (r e)"), ALU.pow).then_inc(pool_route, 1)
                    pool.wait_ge(compared, g + 1)
                    nc.gpsimd.tensor_tensor(same[:], same[:], earlier[:].unsqueeze(1).broadcast_to([P, PAIRS, E, E]),
                                            ALU.mult).then_inc(pool_route, 1)
                    pool.wait_ge(pool_route, 2 * g + 2)
                    nc.gpsimd.tensor_tensor(above[:], above[:], same[:], ALU.add).then_inc(rank_in, 1)

            def add(g, odd, e):
                pool.wait_ge(prod_ready, E * g + e + 1)
                if e >= 2:
                    pool.wait_ge(acc_ready, (E - 1) * g + e - 1)
                nc.gpsimd.tensor_tensor(acc[:, odd, :], acc[:, odd, :], prod[:, e % 2, :], ALU.add).then_inc(acc_ready, 1)

            def experts(g, odd, slot):
                if slot == 1 and not (isinstance(g, int) and g == 0):
                    add(g - 1, 1 - odd, E - 1)
                if slot % CH == 1 and slot // CH >= 2:
                    add(g, odd, slot // CH - 1)
                if slot % 2:
                    pool.wait_ge(h_hi_dve, U // 2 * g + slot // 2 + 1)
                    nc.gpsimd.tensor_tensor(h_lo[:, slot % NH, :], h_full[:, slot % 2, :], f32(h_hi[:, slot % NH, :]),
                                            ALU.subtract).then_inc(h_lo_pool, 1)

            def drain(g):
                add(g - 1, 1, E - 1)

            by_group(pool, attend, experts, drain)

        @block.scalar
        def _(act):
            def attend(g, odd, slot):
                if slot == 3:
                    act.wait_ge(c_turned, g + 1)
                    nc.scalar.copy(cT_hi[:], p_t[:]).then_inc(cT_hi_ready, 1)
                if slot == 5:
                    act.wait_ge(k_made, g + 1)
                    nc.scalar.activation(k_hi[:], p_s[:, 0, :].rearrange("p (r b k) -> p b r k", b=2, k=SEQ),
                                         ACT.Relu).then_inc(k_hi_ready, 1)
                    act.wait_ge(v_made, g + 1)
                    nc.scalar.activation(v_sb[:].rearrange("p r h c -> p (r h c)"), p_m[:], ACT.Relu).then_inc(v_ready, 1)
                if slot == 6:
                    act.wait_ge(x_turned, g + 1)
                    nc.scalar.copy(xT_hi[:], p_t[:]).then_inc(xT_hi_ready, 1)
                if slot == 8:
                    act.wait_ge(q_made, g + 1)
                    nc.scalar.activation(q_hi[:], p_s[:, 1, :].rearrange("p (r b k) -> p b k r", b=2, k=SEQ),
                                         ACT.Relu).then_inc(q_hi_ready, 1)
                if slot == 20:
                    for r in range(PAIRS):
                        act.wait_ge(shifted, PAIRS * g + r + 1)
                        nc.scalar.activation(probs[:, r, :, :], probs[:, r, :, :], ACT.Exp, scale=NORM).then_inc(exp_done, 1)
                if 20 <= slot < 20 + PAIRS:
                    r = slot - 20
                    act.wait_ge(turned, PAIRS * g + r + 1)
                    if r or not (isinstance(g, int) and g == 0):
                        act.wait_ge(av_done, PAIRS * g + r)
                    nc.scalar.copy(probsT[:].rearrange("p t m -> p (t m)"),
                                   p_s[:].rearrange("p s m -> p (s m)")).then_inc(pT_ready, 1)
                if slot == 27:
                    act.wait_ge(x2_turned, g + 1)
                    nc.scalar.copy(x2_hi[:, odd, :], p_t[:]).then_inc(x2_hi_ready, 1)

            def experts(g, odd, slot):
                if slot % CH == 3:
                    e = slot // CH
                    act.wait_ge(wb_made, E * g + e + 1)
                    if e >= 2 or not (isinstance(g, int) and g == 0):
                        act.wait_ge(prod_ready, E * g + e - 1)
                    nc.scalar.copy(wb[:, e % 2, :], p_f[:]).then_inc(wb_ready, 1)
                act.wait_ge(up_done, U * g + slot + 1)
                if slot >= 2 or not (isinstance(g, int) and g == 0):
                    if slot % 2:
                        act.wait_ge(h_lo_pool, U // 2 * g + slot // 2)
                    else:
                        act.wait_ge(h_lo_ready, U // 2 * g + slot // 2)
                nc.scalar.activation(h_full[:, slot % 2, :], p_u[:, slot % 2, :], ACT.Gelu_apprx_tanh).then_inc(h_full_ready, 1)
                if slot % 2 == 0:
                    if slot >= NH or not (isinstance(g, int) and g == 0):
                        act.wait_ge(down_done, U * g + slot - NH + 1)
                    nc.scalar.activation(h_hi[:, slot % NH, :], p_u[:, slot % 2, :], ACT.Gelu_apprx_tanh).then_inc(h_hi_ready, 1)
                if slot == 1:
                    act.wait_ge(wT_turned, g + 1)
                    nc.scalar.copy(wT[0:2 * E, odd, :], p_m[0:2 * E, :]).then_inc(wT_ready, 1)

            by_group(act, attend, experts, lambda g: None)

        @block.vector
        def _(dve):
            nc.vector.memset(f32(q_rows[:]), 0.0).then_inc(zeroed, 1)
            nc.vector.memset(v_rows[:], 0.0).then_inc(zeroed, 1)
            nc.vector.memset(f32(wT[:]), 0.0).then_inc(zeroed, 1)
            dve.wait_ge(zeroed, 3)
            for hp in range(2):
                for r in range(PAIRS):
                    nc.vector.memset(v_rows[64 * hp:64 * hp + 64, r, :, hp, DH * T:], 1.0).then_inc(const_step, 1)
            dve.wait_ge(pool_const, 8)
            nc.vector.tensor_copy(pick[:].rearrange("p e m -> p (e m)"),
                                  probs[:, 0, :, :].rearrange("p h k -> p (h k)")).then_inc(pick_ready, 1)
            dve.wait_ge(w_turned, 1)
            for i in range(3):
                w = p_m[:, i * D:(i + 1) * D]
                w = w.rearrange("p (t h d) -> p h d t", h=2, d=DH) if i == 1 else w.rearrange("p (s j d) -> p s d j", s=S, d=DH)
                to = lambda t: t[:, i, :].rearrange("p (a b c) -> p a b c", a=2, b=DH)
                nc.vector.tensor_copy(to(w_hi), w).then_inc(w_step, 1)
                dve.wait_ge(w_step, i + 1)
                nc.vector.tensor_tensor(to(w_lo), w, f32(to(w_hi)), ALU.subtract).then_inc(w_split_done, 1)
            nc.vector.tensor_copy(r_hi[:], r_raw[:]).then_inc(w_step, 1)
            dve.wait_ge(w_step, 4)
            nc.vector.tensor_tensor(r_lo[:], r_raw[:], f32(r_hi[:]), ALU.subtract).then_inc(w_split_done, 1)
            raw = probs[:].rearrange("p r h k -> p (r h k)")
            for i, (loaded, hi, lo, done) in enumerate(((up_loaded, up_hi, up_lo, up_split), (dn_loaded, dn_hi, dn_lo, dn_split))):
                dve.wait_ge(loaded, 16)
                flat = (lambda t: t[:].rearrange("p e h -> p (e h)")) if i == 0 else (lambda t: t[:].rearrange("p e c d -> p (e c d)"))
                nc.vector.tensor_copy(flat(hi), raw).then_inc(done, 1)
                dve.wait_ge(done, 1)
                nc.vector.tensor_tensor(flat(lo), raw, f32(flat(hi)), ALU.subtract).then_inc(done, 1)
            dve.wait_ge(dn_split, 2)

            def moments(g, k, src):
                for r in range(PAIRS):
                    i = nc.vector.bn_stats(stats[:, r, :], src[:, r, :])
                i.then_inc(ln_step, 1)
                dve.wait_ge(ln_step, 4 * g + 2 * k + 1)
                nc.vector.memset(var_eps[:], 0.0)
                for r in range(PAIRS):
                    i = nc.vector.bn_aggr(mean_var[:, r, :], stats[:, r, :])
                i.then_inc(ln_step, 1)
                dve.wait_ge(ln_step, 4 * g + 2 * k + 2)
                nc.vector.tensor_scalar(var_eps[:], mean_var[:, :, 1], EPS, None, ALU.add).then_inc(var_ready, 1)

            def normalise(g, k, src):
                dve.wait_ge(rstd_ready, 2 * g + k + 1)
                for r in range(PAIRS):
                    i = nc.vector.tensor_scalar(xn[:, r, :], src[:, r, :], mean_var[:, r, 0:1], rstd[:, r:r + 1],
                                                ALU.subtract, ALU.mult)
                i.then_inc(xn_ready, 1)

            def attend(g, odd, slot):
                if slot == 2:
                    dve.wait_ge(x_loaded, 16 * (g + 1))
                    moments(g, 0, x_in)
                if slot == 3:
                    dve.wait_ge(cT_hi_ready, g + 1)
                    nc.vector.tensor_tensor(cT_lo[:], p_t[:], f32(cT_hi[:]), ALU.subtract).then_inc(cT_lo_ready, 1)
                    if not (isinstance(g, int) and g == 0):
                        dve.wait_ge(x2_turned, g)
                    normalise(g, 0, x_in)
                if slot == 5:
                    dve.wait_ge(k_hi_ready, g + 1)
                    for b in range(2):
                        i = nc.vector.scalar_tensor_tensor(
                            out=k_lo[:, b, :, :], in0=p_s[:, 0, :].rearrange("p (r b k) -> p b r k", b=2, k=SEQ)[:, b, :, :],
                            scalar=0.0, in1=f32(k_hi[:, b, :, :]), op0=ALU.max, op1=ALU.subtract)
                    i.then_inc(k_lo_ready, 1)
                if slot == 6:
                    dve.wait_ge(xT_hi_ready, g + 1)
                    nc.vector.tensor_tensor(xT_lo[:], p_t[:], f32(xT_hi[:]), ALU.subtract).then_inc(xT_lo_ready, 1)
                if slot == 8:
                    dve.wait_ge(q_hi_ready, g + 1)
                    nc.vector.scalar_tensor_tensor(
                        out=q_lo[:].rearrange("p b k r -> p (b k) r"), in0=p_s[:, 1, :].rearrange("p (r m) -> p m r", r=PAIRS),
                        scalar=0.0, in1=f32(q_hi[:]).rearrange("p b k r -> p (b k) r"), op0=ALU.max,
                        op1=ALU.subtract).then_inc(q_lo_ready, 1)
                if 12 <= slot < 12 + 2 * PAIRS:
                    r = (slot - 12) // 2
                    sc = p_s[:].rearrange("p s (j k) -> p (s j) k", k=SEQ)
                    if slot % 2 == 0:
                        dve.wait_ge(scores_ready, PAIRS * g + r + 1)
                        nc.vector.tensor_reduce(row_max[:], sc, AX.X, ALU.max).then_inc(max_ready, 1)
                    else:
                        dve.wait_ge(max_ready, PAIRS * g + r + 1)
                        nc.vector.tensor_tensor(probs[:, r, :, :], sc, row_max[:].unsqueeze(2).broadcast_to([P, HEADS, SEQ]),
                                                ALU.subtract).then_inc(shifted, 1)
                if 21 <= slot < 21 + PAIRS:
                    r = slot - 21
                    dve.wait_ge(av_done, PAIRS * g + r + 1)
                    o = p_m[:, 0:T * 4 * (DH + 1)].rearrange("p (t b h d) -> p b t h d", t=T, b=2, h=2)
                    inv = inv_sum[:].rearrange("p (t h) -> p t h", h=2)
                    for b in range(2):
                        rows = slice(64 * b, 64 * b + 64)
                        i = nc.vector.reciprocal(inv[rows], o[rows, b, :, :, DH])
                    i.then_inc(sums_ready, 1)
                    dve.wait_ge(sums_ready, PAIRS * g + r + 1)
                    for b in range(2):
                        rows = slice(64 * b, 64 * b + 64)
                        i = nc.vector.tensor_tensor(att[rows].rearrange("p (t h) d -> p t h d", h=2), o[rows, b, :, :, 0:DH],
                                                    inv[rows].unsqueeze(3).broadcast_to([64, T, 2, DH]), ALU.mult)
                    i.then_inc(o_read, 1)
                    dve.wait_ge(o_read, PAIRS * g + r + 1)
                    nc.vector.tensor_tensor(x1[:, odd, r, :], x_in[:, r, :], att[:].rearrange("p h d -> p (h d)"),
                                            ALU.add).then_inc(x1_ready, 1)
                if slot == 25:
                    dve.wait_ge(x1_ready, PAIRS * (g + 1))
                    moments(g, 1, x1[:, odd])
                if slot == 26:
                    dve.wait_ge(x_turned, g + 1)
                    normalise(g, 1, x1[:, odd])
                if slot == 27:
                    dve.wait_ge(x2_hi_ready, g + 1)
                    nc.vector.tensor_tensor(x2_lo[:, odd, :], p_t[:], f32(x2_hi[:, odd, :]), ALU.subtract).then_inc(x2_lo_ready, 1)
                if slot == 29:
                    dve.wait_ge(logits_ready, g + 1)
                    lg = p_m[:, 0:PAIRS * E].rearrange("p (r e) -> p r e", e=E)
                    nc.vector.tensor_reduce(logit_max[:], lg, AX.X, ALU.max).then_inc(route_step, 1)
                    dve.wait_ge(route_step, 6 * g + 1)
                    nc.vector.tensor_tensor(logits[:], lg, logit_max[:].unsqueeze(2).broadcast_to([P, PAIRS, E]),
                                            ALU.subtract).then_inc(logits_read, 1)
                if slot == 30:
                    dve.wait_ge(pool_route, 2 * g + 1)
                    other = expert_p[:].unsqueeze(2).broadcast_to([P, PAIRS, E, E])
                    own = expert_p[:].unsqueeze(3).broadcast_to([P, PAIRS, E, E])
                    nc.vector.tensor_tensor(above[:], other, own, ALU.is_gt)
                    nc.vector.tensor_tensor(same[:], other, own, ALU.is_equal).then_inc(compared, 1)
                if slot == 31:
                    dve.wait_ge(rank_in, g + 1)
                    nc.vector.tensor_reduce(rank[:], above[:], AX.X, ALU.add).then_inc(route_step, 1)
                    dve.wait_ge(route_step, 6 * g + 2)
                    nc.vector.scalar_tensor_tensor(out=w_sel[:].rearrange("p r e -> p (r e)"), in0=rank[:].rearrange("p r e -> p (r e)"),
                                                   scalar=TOPK - 0.5, in1=expert_p[:].rearrange("p r e -> p (r e)"),
                                                   op0=ALU.is_lt, op1=ALU.mult).then_inc(route_step, 1)
                    dve.wait_ge(route_step, 6 * g + 3)
                    nc.vector.tensor_reduce(w_sum[:], w_sel[:], AX.X, ALU.add).then_inc(route_step, 1)
                    dve.wait_ge(route_step, 6 * g + 4)
                    nc.vector.reciprocal(w_inv[:], w_sum[:]).then_inc(route_step, 1)
                    dve.wait_ge(route_step, 6 * g + 5)
                    nc.vector.tensor_tensor(w_norm[:], w_sel[:], w_inv[:].unsqueeze(2).broadcast_to([P, PAIRS, E]),
                                            ALU.mult).then_inc(route_step, 1)
                    dve.wait_ge(route_step, 6 * g + 6)
                    nc.vector.tensor_copy(w_round[:], w_norm[:]).then_inc(round_done, 1)
                    dve.wait_ge(round_done, g + 1)
                    nc.vector.tensor_copy(w_split[:, :, 0, :], f32(w_round[:]))
                    nc.vector.tensor_tensor(w_split[:, :, 1, :], w_norm[:], f32(w_round[:]), ALU.subtract).then_inc(weights_ready, 1)

            def weigh(g, odd, e):
                dve.wait_ge(down_done, U * g + CH * (e + 1))
                dve.wait_ge(wb_ready, E * g + e + 1)
                if e >= 3:
                    dve.wait_ge(acc_ready, (E - 1) * g + e - 2)
                elif e in (1, 2) and not (isinstance(g, int) and g == 0):
                    dve.wait_ge(acc_ready, (E - 1) * g)
                to = acc[:, odd, :] if e == 0 else prod[:, e % 2, :]
                nc.vector.tensor_tensor(to, p_y[:], wb[:, e % 2, :], ALU.mult).then_inc(prod_ready, 1)

            def residual(g, odd):
                dve.wait_ge(out_turned, g + 1)
                if not (isinstance(g, int) and g == 0):
                    dve.wait_ge(stored, 16 * g)
                nc.vector.tensor_tensor(o_sb[:].rearrange("p r d -> p (r d)"), p_f[:],
                                        x1[:, odd].rearrange("p r d -> p (r d)"), ALU.add).then_inc(out_ready, 1)

            def experts(g, odd, slot):
                first = isinstance(g, int) and g == 0
                if slot % CH == 1:
                    if slot > CH:
                        weigh(g, odd, slot // CH - 1)
                    elif not first:
                        weigh(g - 1, 1 - odd, E - 1)
                dve.wait_ge(h_full_ready, U * g + slot + 1)
                if slot % 2:
                    if slot >= NH or not first:
                        dve.wait_ge(down_done, U * g + slot - NH + 1)
                    nc.vector.tensor_copy(h_hi[:, slot % NH, :], h_full[:, slot % 2, :]).then_inc(h_hi_dve, 1)
                else:
                    dve.wait_ge(h_hi_ready, U // 2 * g + slot // 2 + 1)
                    nc.vector.tensor_tensor(h_lo[:, slot % NH, :], h_full[:, slot % 2, :], f32(h_hi[:, slot % NH, :]),
                                            ALU.subtract).then_inc(h_lo_ready, 1)
                if slot == 6 and not first:
                    residual(g - 1, 1 - odd)

            def drain(g):
                weigh(g - 1, 1, E - 1)
                residual(g - 1, 1)

            by_group(dve, attend, experts, drain)

        @block.tensor
        def _(pe):
            pe.wait_ge(w_loaded, 64)
            pe.wait_ge(pool_const, 5)
            for i in range(3):
                mm = nc.tensor.transpose(p_m[:, i * D:(i + 1) * D], w_raw[:, i, :], ident[:])
            mm.then_inc(w_turned, 1)
            pe.wait_ge(w_split_done, 4)

            def three(out, lhs_hi, lhs_lo, rhs_hi, rhs_lo, start=True, stop=True):
                nc.tensor.matmul(out, lhs_hi, rhs_hi, start=start, stop=False)
                nc.tensor.matmul(out, lhs_hi, rhs_lo, start=False, stop=False)
                return nc.tensor.matmul(out, lhs_lo, rhs_hi, start=False, stop=stop)

            def turn(bank, src):
                for r in range(4):
                    mm = nc.tensor.transpose(bank[:, r * P:(r + 1) * P], src[:, r, :], ident[:])
                return mm

            def attend(g, odd, slot):
                first = isinstance(g, int) and g == 0
                if slot == 2:
                    pe.wait_ge(c_loaded, 16 * (g + 1))
                    if not first:
                        pe.wait_ge(x2_hi_ready, g)
                        pe.wait_ge(x2_lo_ready, g)
                    turn(p_t, c_in).then_inc(c_turned, 1)
                if slot == 4:
                    pe.wait_ge(cT_hi_ready, g + 1)
                    pe.wait_ge(cT_lo_ready, g + 1)
                    if not first:
                        pe.wait_ge(pT_ready, PAIRS * g)
                        pe.wait_ge(wT_ready, g)
                    three(p_s[:, 0, :], w_hi[:, 0, :], w_lo[:, 0, :], cT_hi[:], cT_lo[:]).then_inc(k_made, 1)
                    for r in range(PAIRS):
                        tok = slice(r * P, (r + 1) * P)
                        mm = three(p_m[:, tok], cT_hi[:, tok], cT_lo[:, tok], w_hi[:, 1, :], w_lo[:, 1, :])
                    mm.then_inc(v_made, 1)
                if slot == 5:
                    pe.wait_ge(xn_ready, 2 * g + 1)
                    turn(p_t, xn).then_inc(x_turned, 1)
                if slot == 7:
                    pe.wait_ge(xT_hi_ready, g + 1)
                    pe.wait_ge(xT_lo_ready, g + 1)
                    three(p_s[:, 1, :], w_hi[:, 2, :], w_lo[:, 2, :], xT_hi[:], xT_lo[:]).then_inc(q_made, 1)
                if 12 <= slot < 12 + 2 * PAIRS and slot % 2 == 0:
                    r = (slot - 12) // 2
                    if r == 0:
                        pe.wait_ge(k_placed, 16 * 2 * S * PARTS * (g + 1))
                        pe.wait_ge(q_placed, 16 * 2 * S * PARTS * (g + 1))
                    else:
                        pe.wait_ge(shifted, PAIRS * g + r)
                    for j in range(J):
                        for s in range(S):
                            rows = slice(64 * s, 64 * s + 64)
                            mm = nc.tensor.matmul(p_s[:, s, j * SEQ:(j + 1) * SEQ], q_rows[rows, j, :, r],
                                                  k_rows[rows, j, r, :], start=True, stop=True)
                    mm.then_inc(scores_ready, 1)
                if 21 <= slot < 21 + PAIRS:
                    r = slot - 21
                    pe.wait_ge(pT_ready, PAIRS * g + r + 1)
                    if r == 0:
                        pe.wait_ge(v_placed, 16 * 4 * (g + 1))
                    else:
                        pe.wait_ge(o_read, PAIRS * g + r)
                    vr = v_rows[:, r, :, :, :].rearrange("p b h (d t) -> p (b h) d t", t=T)
                    w = 4 * (DH + 1)
                    for t in range(T):
                        mm = nc.tensor.matmul(p_m[:, t * w:(t + 1) * w], probsT[:, t, :], vr[:, :, :, t], start=True, stop=True)
                    mm.then_inc(av_done, 1)
                if 20 <= slot < 20 + PAIRS:
                    r = slot - 20
                    if r == 0:
                        pe.wait_ge(shifted, PAIRS * (g + 1))
                    pe.wait_ge(exp_done, PAIRS * g + r + 1)
                    for t in range(T):
                        mm = nc.tensor.transpose(p_s[:, t // 4, t % 4 * P:(t % 4 + 1) * P],
                                                 probs[:, r, 2 * t:2 * t + 2, :].rearrange("p h k -> p (h k)"), ident[:])
                    mm.then_inc(turned, 1)
                if slot == 27:
                    pe.wait_ge(xn_ready, 2 * g + 2)
                    turn(p_t, xn).then_inc(x2_turned, 1)
                if slot == 28:
                    pe.wait_ge(x2_hi_ready, g + 1)
                    pe.wait_ge(x2_lo_ready, g + 1)
                    pe.wait_ge(o_read, PAIRS * (g + 1))
                    for r in range(PAIRS):
                        tok = slice(r * P, (r + 1) * P)
                        mm = three(p_m[:, r * E:(r + 1) * E], x2_hi[:, odd, tok], x2_lo[:, odd, tok], r_hi[:], r_lo[:])
                    mm.then_inc(logits_ready, 1)

            def down(g, unit):
                e, c = unit // CH, unit % CH
                if unit % 2:
                    pe.wait_ge(h_hi_dve, U // 2 * g + unit // 2 + 1)
                    pe.wait_ge(h_lo_pool, U // 2 * g + unit // 2 + 1)
                else:
                    pe.wait_ge(h_hi_ready, U // 2 * g + unit // 2 + 1)
                    pe.wait_ge(h_lo_ready, U // 2 * g + unit // 2 + 1)
                if c == 0 and not (isinstance(g, int) and g == 0 and e == 0):
                    pe.wait_ge(prod_ready, E * g + e)
                three(p_y[:], dn_hi[:, e, c, :], dn_lo[:, e, c, :], h_hi[:, unit % NH, :], h_lo[:, unit % NH, :],
                      start=(c == 0), stop=(c == CH - 1)).then_inc(down_done, 1)

            def turn_out(g, odd, n):
                pe.wait_ge(acc_ready, (E - 1) * (g + 1))
                pe.wait_ge(wb_ready, n)
                for r in range(PAIRS):
                    mm = nc.tensor.transpose(p_f[:, r * P:(r + 1) * P], acc[:, odd, r * P:(r + 1) * P], ident[:])
                mm.then_inc(out_turned, 1)

            def experts(g, odd, slot):
                first = isinstance(g, int) and g == 0
                e, c = slot // CH, slot % CH
                if slot == 0:
                    pe.wait_ge(x2_lo_ready, g + 1)
                    pe.wait_ge(x2_hi_ready, g + 1)
                    if first:
                        pe.wait_ge(dn_split, 2)
                if slot >= 2 or not first:
                    if slot % 2:
                        pe.wait_ge(h_full_ready, U * g + slot - 1)
                    else:
                        pe.wait_ge(h_hi_ready, U // 2 * g + slot // 2)
                hid = slice(c * P, (c + 1) * P)
                three(p_u[:, slot % 2, :], up_hi[:, e, hid], up_lo[:, e, hid], x2_hi[:, odd, :], x2_lo[:, odd, :]).then_inc(up_done, 1)
                if slot >= LAG:
                    down(g, slot - LAG)
                elif not first:
                    down(g - 1, U + slot - LAG)
                if slot == 1:
                    pe.wait_ge(weights_ready, g + 1)
                    for r in range(PAIRS):
                        mm = nc.tensor.transpose(p_m[0:2 * E, r * P:(r + 1) * P],
                                                 w_split[:, r, :, :].rearrange("p a e -> p (a e)"), ident[:])
                    mm.then_inc(wT_turned, 1)
                if c == 2:
                    if e == 0:
                        pe.wait_ge(wT_ready, g + 1)
                    if e == 1 and not first:
                        pe.wait_ge(out_ready, g)
                    if e or not first:
                        pe.wait_ge(wb_ready, E * g + e)
                    nc.tensor.matmul(p_f[:], pick[:, e, :], wT[:, odd, :], start=True, stop=True).then_inc(wb_made, 1)
                if slot == 4 and not first:
                    turn_out(g - 1, 1 - odd, E * g + 1)

            def drain(g):
                for unit in range(U - LAG, U):
                    down(g - 1, unit)
                turn_out(g - 1, 1, E * g)

            by_group(pe, attend, experts, drain)


_INS = ['x', 'ctx_1024', 'L0_xattn_Wq', 'L0_xattn_Wk', 'L0_xattn_Wv', 'L0_ffn_router_w', 'L0_ffn_up_w', 'L0_ffn_down_w']
_OUTS = [((128, 64, 128), 'float32')]


def kernel(**inputs):
    import numpy as _np
    import concourse.bacc as _bacc
    from concourse import mybir as _mybir
    from concourse.bass_utils import run_bass_kernel_spmd as _run

    nc = _bacc.Bacc("TRN2", target_bir_lowering=False, num_devices=1)
    arrays, args = {}, []
    for name in _INS:
        a = _np.ascontiguousarray(inputs[name])
        arrays[f"in_{name}_dram"] = a
        args.append(nc.dram_tensor(f"in_{name}_dram", a.shape, _mybir.dt.from_np(a.dtype), kind="ExternalInput").ap())
    for i, (shape, dtype) in enumerate(_OUTS):
        dt = _mybir.dt.from_np(_np.dtype(dtype))
        args.append(nc.dram_tensor(f"out_{i}_dram", shape, dt, kind="ExternalOutput").ap())
    build(nc, *args)
    r = _run(nc, [arrays], core_ids=[0])
    return r.results[0]["out_0_dram"]
```

```python
from contextlib import ExitStack

import concourse.bass as bass
from concourse import mybir

F32 = mybir.dt.float32
F32R = mybir.dt.float32r
ALU = mybir.AluOpType
ACT = mybir.ActivationFunctionType
AX = mybir.AxisListType

P = 128
HEADS = 16
TOPK = 4
EPS = 1e-5
E_BASE = 2.718281828459045


def build(nc, x, ctx_in, wq, wk, wv, router_w, up_w, down_w, out):
    NSEQ, SEQ, D = x.shape
    _, _, HID = up_w.shape
    E = router_w.shape[1]
    DH = D // HEADS
    NORM = float(DH) ** -0.5
    PAIR = 2 * SEQ
    TOK = 512
    PAIRS = TOK // PAIR
    G = NSEQ * SEQ // TOK
    S = 2
    J = HEADS // S
    PARTS = 4
    T = HEADS // 2
    CH = HID // P
    U = E * CH
    HALF = PAIRS * SEQ
    LAG = 3
    TURN_C, NORM1, V_OUT, TURN_X, K_OUT, Q_OUT, V_MOVE = 1, 2, 3, 8, 10, 12, 18
    SCORE_EVERY = 3
    EXP = SCORE_EVERY * PAIRS
    NORM2, TURN_X2, ROUTE = 18, 21, 23
    POWERS = (25, 26, 27, 29)
    W_TURN, OUT = 2, 6
    NH = 4
    POOL_LOW = [slot for slot in range(U) if (slot % 2 and slot not in POWERS) or slot in (6, 10)]
    DVE_LOW = [slot for slot in range(U) if slot not in POOL_LOW]
    assert PAIR == P and D == P and S * 2 * PARTS * DH == P and G % 2 == 0

    x_v = x.rearrange("(g r b) s d -> g (b s) r d", r=PAIRS, b=2)
    c_v = ctx_in.rearrange("(g r b) s d -> g (b s) r d", r=PAIRS, b=2)
    o_v = out.rearrange("(g r b) s d -> g (b s) r d", r=PAIRS, b=2)

    with ExitStack() as stack:
        def sb(name, shape, dt=F32):
            return stack.enter_context(nc.sbuf_tensor(name, shape, dt))

        def ps(name, shape):
            return stack.enter_context(nc.psum_tensor(name, shape, F32))

        def sem(name):
            return stack.enter_context(nc.semaphore(name))

        up_hi = sb("up_hi", [P, E, HID], F32R)
        up_lo = sb("up_lo", [P, E, HID], F32R)
        dn_hi = sb("dn_hi", [P, E, CH, D], F32R)
        dn_lo = sb("dn_lo", [P, E, CH, D], F32R)
        w_hi = sb("w_hi", [P, 3, D], F32R)
        w_lo = sb("w_lo", [P, 3, D], F32R)
        r_raw = sb("r_raw", [P, E])
        r_hi = sb("r_hi", [P, E], F32R)
        r_lo = sb("r_lo", [P, E], F32R)
        ident = sb("ident", [P, P])
        pick = sb("pick", [P, E, P], F32R)
        earlier = sb("earlier", [P, E, E])
        minus_half = sb("minus_half", [P, PAIRS])
        e_base = sb("e_base", [P, E])
        x_in = sb("x_in", [P, 2, PAIRS, D])
        c_in = sb("c_in", [P, PAIRS, D])
        stats = sb("stats", [P, PAIRS, 6])
        mean_var = sb("mean_var", [P, PAIRS, 2])
        var_eps = sb("var_eps", [P, PAIRS])
        rstd = sb("rstd", [P, PAIRS])
        xn = sb("xn", [P, PAIRS, D])
        cT_hi = sb("cT_hi", [P, TOK], F32R)
        cT_lo = sb("cT_lo", [P, TOK], F32R)
        xT_hi = sb("xT_hi", [P, TOK], F32R)
        xT_lo = sb("xT_lo", [P, TOK], F32R)
        q_hi = sb("q_hi", [P, 2, SEQ, PAIRS], F32R)
        q_lo = sb("q_lo", [P, 2, SEQ, PAIRS], F32R)
        k_hi = sb("k_hi", [P, 2, PAIRS, SEQ], F32R)
        k_lo = sb("k_lo", [P, 2, PAIRS, SEQ], F32R)
        v_sb = sb("v_sb", [P, PAIRS, 2, DH * T])
        q_rows = sb("q_rows", [P, J, 2 * SEQ, PAIRS], F32R)
        k_rows = sb("k_rows", [P, J, S, PAIRS, SEQ], F32R)
        v_rows = sb("v_rows", [P, PAIRS, 2, 2, (DH + 1) * T])
        row_max = sb("row_max", [P, HEADS])
        probs = sb("probs", [P, PAIRS, HEADS, SEQ])
        probsT = sb("probsT", [P, T, P])
        inv_sum = sb("inv_sum", [P, HEADS])
        att = sb("att", [P, HEADS, DH])
        x1 = sb("x1", [P, 2, PAIRS, D])
        x2_hi = sb("x2_hi", [P, 2, TOK], F32R)
        x2_lo = sb("x2_lo", [P, 2, TOK], F32R)
        wT = sb("wT", [P, TOK], F32R)
        logit_max = sb("logit_max", [P, PAIRS])
        logits = sb("logits", [P, PAIRS, E])
        expert_p = sb("expert_p", [P, PAIRS, E])
        above = sb("above", [P, PAIRS, E, E])
        same = sb("same", [P, PAIRS, E, E])
        rank = sb("rank", [P, PAIRS, E])
        w_sel = sb("w_sel", [P, PAIRS, E])
        w_sum = sb("w_sum", [P, PAIRS])
        w_inv = sb("w_inv", [P, PAIRS])
        w_norm = sb("w_norm", [P, PAIRS, E])
        w_round = sb("w_round", [P, PAIRS, E], F32R)
        w_split = sb("w_split", [P, PAIRS, 2, E])
        h_full = sb("h_full", [P, NH, TOK])
        w_raw = h_full[:].rearrange("p a m -> p (a m)")[:, 0:3 * D].rearrange("p (i d) -> p i d", i=3)
        h_hi = sb("h_hi", [P, NH, TOK], F32R)
        h_lo = sb("h_lo", [P, NH, TOK], F32R)
        wb = sb("wb", [P, TOK])
        prod = sb("prod", [P, 2, TOK])
        acc = sb("acc", [P, TOK])
        o_sb = sb("o_sb", [P, PAIRS, D])

        p_s = ps("p_s", [P, 2, 512])
        p_t = ps("p_t", [P, 512])
        p_m = ps("p_m", [P, 512])
        p_u = ps("p_u", [P, 2, 512])
        p_y = ps("p_y", [P, 2, 512])

        up_loaded = sem("up_loaded")
        dn_loaded = sem("dn_loaded")
        w_loaded = sem("w_loaded")
        x_loaded = sem("x_loaded")
        c_loaded = sem("c_loaded")
        q_placed = sem("q_placed")
        k_placed = sem("k_placed")
        v_placed = sem("v_placed")
        stored = sem("stored")
        pool_const = sem("pool_const")
        zeroed = sem("zeroed")
        w_turned = sem("w_turned")
        const_step = sem("const_step")
        w_step = sem("w_step")
        up_split = sem("up_split")
        dn_split = sem("dn_split")
        w_split_done = sem("w_split_done")
        pick_ready = sem("pick_ready")
        var_ready = [sem(f"var_ready_{k}") for k in (1, 2)]
        rstd_ready = [sem(f"rstd_ready_{k}") for k in (1, 2)]
        ln_step = [sem(f"ln_step_{k}") for k in (1, 2)]
        xn_ready = [sem(f"xn_ready_{k}") for k in (1, 2)]
        c_turned = sem("c_turned")
        x_turned = sem("x_turned")
        cT_hi_ready = sem("cT_hi_ready")
        cT_lo_ready = sem("cT_lo_ready")
        xT_hi_ready = sem("xT_hi_ready")
        xT_lo_ready = sem("xT_lo_ready")
        k_made = sem("k_made")
        v_made = sem("v_made")
        q_made = sem("q_made")
        k_hi_ready = sem("k_hi_ready")
        k_lo_ready = sem("k_lo_ready")
        v_ready = sem("v_ready")
        q_hi_ready = sem("q_hi_ready")
        q_lo_ready = sem("q_lo_ready")
        scores_ready = sem("scores_ready")
        max_ready = sem("max_ready")
        shifted = sem("shifted")
        exp_done = sem("exp_done")
        turned = sem("turned")
        pT_ready = sem("pT_ready")
        av_done = sem("av_done")
        sums_ready = sem("sums_ready")
        o_read = sem("o_read")
        x1_ready = sem("x1_ready")
        x2_turned = sem("x2_turned")
        x2_hi_ready = sem("x2_hi_ready")
        x2_lo_ready = sem("x2_lo_ready")
        logits_ready = sem("logits_ready")
        route_step = sem("route_step")
        logits_read = sem("logits_read")
        powers = sem("powers")
        ties_marked = sem("ties_marked")
        rank_in = sem("rank_in")
        weights_ready = sem("weights_ready")
        wT_turned = sem("wT_turned")
        round_done = sem("round_done")
        compared = sem("compared")
        wT_ready = sem("wT_ready")
        wb_made = sem("wb_made")
        wb_ready = sem("wb_ready")
        up_done = sem("up_done")
        h_full_ready = sem("h_full_ready")
        h_hi_ready = sem("h_hi_ready")
        h_hi_dve = sem("h_hi_dve")
        h_lo_ready = sem("h_lo_ready")
        h_lo_pool = sem("h_lo_pool")
        down_done = sem("down_done")
        prod_ready = sem("prod_ready")
        acc_ready = sem("acc_ready")
        out_turned = sem("out_turned")
        out_ready = sem("out_ready")

        block = stack.enter_context(nc.Block())

        def f32(ap):
            return ap.bitcast(F32)

        def raw_weights():
            return probs[:].rearrange("p r h k -> p (r h k)")

        def by_group(eng, front, back, experts, drain):
            def step(g, odd, with_experts, with_back, with_front):
                for slot in range(U):
                    if with_experts:
                        experts(g, odd, slot)
                    if with_back:
                        back(g + 1, 1 - odd, slot, with_front)
                    if with_front:
                        front(g + 2, odd, slot)

            step(-2, 0, False, False, True)
            step(-1, 1, False, True, True)
            step(0, 0, True, True, True)
            with eng.Fori(0, (G - 4) // 2) as i:
                step(2 * i + 1, 1, True, True, True)
                step(2 * i + 2, 0, True, True, True)
            step(G - 3, 1, True, True, True)
            step(G - 2, 0, True, True, False)
            step(G - 1, 1, True, False, False)
            drain(G)

        def low_done(eng, g, slot):
            if slot < 0:
                g, slot = g - 1, slot + U
            if slot in POOL_LOW:
                eng.wait_ge(h_lo_pool, len(POOL_LOW) * g + POOL_LOW.index(slot) + 1)
            else:
                eng.wait_ge(h_lo_ready, len(DVE_LOW) * g + DVE_LOW.index(slot) + 1)

        def begun(g, n=1):
            return not isinstance(g, int) or g >= n

        @block.sync
        def _(sp):
            for i, w in enumerate((wk, wv, wq)):
                sp.dma_start(w_raw[:, i, :], w).then_inc(w_loaded, 16)
            sp.dma_start(r_raw[:], router_w).then_inc(w_loaded, 16)

            def spread(rows_of, placed):
                for s in range(S):
                    for b in range(2):
                        for part in range(PARTS):
                            row = 2 * PARTS * DH * s + PARTS * DH * b + DH * part
                            to, src = rows_of(s, b, part, slice(row, row + DH))
                            sp.dma_start(f32(to), f32(src[64 * s:64 * s + 64, b, :, :])).then_inc(placed, 16)

            def load_x_c(g, odd):
                if begun(g):
                    sp.wait_ge(c_turned, g)
                sp.dma_start(c_in[:], c_v[g]).then_inc(c_loaded, 16)
                if begun(g, 2):
                    sp.wait_ge(x1_ready, PAIRS * (g - 1))
                sp.dma_start(x_in[:, odd], x_v[g]).then_inc(x_loaded, 16)

            def front(g, odd, slot):
                if slot == 0 and not begun(g):
                    load_x_c(0, 0)
                    sp.wait_ge(pick_ready, 1)
                    sp.dma_start(raw_weights().rearrange("p (e h) -> p e h", e=E),
                                 up_w.rearrange("e d h -> d e h")).then_inc(up_loaded, 16)
                if slot == K_OUT + 1:
                    if not begun(g):
                        sp.wait_ge(zeroed, 4)
                    sp.wait_ge(k_hi_ready, g + 1)
                    sp.wait_ge(k_lo_ready, g + 1)
                    spread(lambda s, b, part, rows: (k_rows[rows, :, s, :, :], (k_hi, k_lo)[part % 2]), k_placed)
                if slot == Q_OUT + 1:
                    sp.wait_ge(q_hi_ready, g + 1)
                    sp.wait_ge(q_lo_ready, g + 1)
                    spread(lambda s, b, part, rows: (q_rows[rows, :, SEQ * b:SEQ * b + SEQ, :], (q_hi, q_lo)[part // 2]), q_placed)
                if slot == V_MOVE:
                    if begun(g):
                        sp.wait_ge(av_done, PAIRS * g)
                    for hp in range(2):
                        for b in range(2):
                            sp.dma_start(v_rows[64 * hp:64 * hp + 64, :, b, hp, 0:DH * T],
                                         v_sb[64 * b:64 * b + 64, :, hp, :]).then_inc(v_placed, 16)
                    if not (isinstance(g, int) and g == G - 1):
                        load_x_c(g + 1, 1 - odd)
                    if not begun(g):
                        sp.wait_ge(up_split, 2)
                        sp.dma_start(raw_weights().rearrange("p (e c d) -> p e c d", e=E, c=CH),
                                     down_w.rearrange("e (c p) d -> p e c d", p=P)).then_inc(dn_loaded, 16)

            def back(g, odd, slot, beside):
                pass

            def store(g):
                sp.wait_ge(out_ready, g + 1)
                sp.dma_start(o_v[g], o_sb[:]).then_inc(stored, 16)

            def experts(g, odd, slot):
                if slot == OUT + 1 and begun(g):
                    store(g - 1)

            def drain(g):
                store(g - 1)
                sp.wait_ge(stored, 16 * G)

            by_group(sp, front, back, experts, drain)

        @block.gpsimd
        def _(pool):
            sel = probs[:, 0, :, :].rearrange("p h k -> p (h k)").rearrange("p (e m) -> p e m", e=E)
            nc.gpsimd.memset(ident[:], 0.0).then_inc(pool_const, 1)
            nc.gpsimd.memset(earlier[:], 1.0).then_inc(pool_const, 1)
            nc.gpsimd.memset(sel, 0.0).then_inc(pool_const, 1)
            nc.gpsimd.memset(minus_half[:], -0.5)
            nc.gpsimd.memset(e_base[:], E_BASE).then_inc(pool_const, 1)
            pool.wait_ge(pool_const, 4)
            nc.gpsimd.affine_select(out=ident[:], in_=ident[:], compare_op=ALU.not_equal, fill=1.0, base=0,
                                    pattern=[[-1, P]], channel_multiplier=1).then_inc(pool_const, 1)
            nc.gpsimd.affine_select(out=earlier[:], in_=earlier[:], compare_op=ALU.is_gt, fill=0.0, base=0,
                                    pattern=[[1, E], [-1, E]], channel_multiplier=0).then_inc(pool_const, 1)
            nc.gpsimd.affine_select(out=sel, in_=sel, compare_op=ALU.not_equal, fill=1.0, base=0,
                                    pattern=[[-1, E], [0, P]], channel_multiplier=1).then_inc(pool_const, 1)
            pool.wait_ge(pool_const, 7)
            nc.gpsimd.affine_select(out=sel, in_=sel, compare_op=ALU.not_equal, fill=1.0, base=-E,
                                    pattern=[[-1, E], [0, P]], channel_multiplier=1).then_inc(pool_const, 1)

            def inv_root(g, k):
                pool.wait_ge(var_ready[k], g + 1)
                nc.gpsimd.tensor_tensor(rstd[:], var_eps[:], minus_half[:], ALU.pow).then_inc(rstd_ready[k], 1)

            def front(g, odd, slot):
                if slot == NORM1:
                    inv_root(g, 0)

            def back(g, odd, slot, beside):
                if slot == NORM2:
                    inv_root(g, 1)
                if slot in POWERS:
                    r = POWERS.index(slot)
                    pool.wait_ge(logits_read, g + 1)
                    nc.gpsimd.tensor_tensor(expert_p[:, r, :], e_base[:], logits[:, r, :], ALU.pow).then_inc(powers, 1)
                if slot == ROUTE + 3:
                    pool.wait_ge(compared, g + 1)
                    nc.gpsimd.tensor_tensor(same[:], same[:], earlier[:].unsqueeze(1).broadcast_to([P, PAIRS, E, E]),
                                            ALU.mult).then_inc(ties_marked, 1)
                    pool.wait_ge(ties_marked, g + 1)
                    nc.gpsimd.tensor_tensor(above[:], above[:], same[:], ALU.add).then_inc(rank_in, 1)

            def add(g, odd, e):
                pool.wait_ge(prod_ready, E * g + e + 1)
                if e >= 2:
                    pool.wait_ge(acc_ready, (E - 1) * g + e - 1)
                nc.gpsimd.tensor_tensor(acc[:], acc[:], prod[:, e % 2, :], ALU.add).then_inc(acc_ready, 1)

            def experts(g, odd, slot):
                if slot in (0, CH) and begun(g):
                    add(g - 1, 1 - odd, E - 2 + slot // CH)
                if slot % CH == 0 and slot // CH >= 3:
                    add(g, odd, slot // CH - 2)
                if slot in POOL_LOW:
                    if slot % 2:
                        pool.wait_ge(h_hi_dve, U // 2 * g + slot // 2 + 1)
                    else:
                        pool.wait_ge(h_hi_ready, U // 2 * g + slot // 2 + 1)
                    nc.gpsimd.tensor_tensor(h_lo[:, slot % NH, :], h_full[:, slot % NH, :], f32(h_hi[:, slot % NH, :]),
                                            ALU.subtract).then_inc(h_lo_pool, 1)

            def drain(g):
                add(g - 1, 1, E - 2)
                add(g - 1, 1, E - 1)

            by_group(pool, front, back, experts, drain)

        @block.scalar
        def _(act):
            def front(g, odd, slot):
                if slot == TURN_C:
                    act.wait_ge(c_turned, g + 1)
                    nc.scalar.copy(cT_hi[:], p_t[:]).then_inc(cT_hi_ready, 1)
                if slot == TURN_X:
                    act.wait_ge(x_turned, g + 1)
                    nc.scalar.copy(xT_hi[:], p_t[:]).then_inc(xT_hi_ready, 1)
                if slot == V_OUT:
                    if begun(g):
                        act.wait_ge(v_placed, 16 * 4 * g)
                    act.wait_ge(v_made, g + 1)
                    nc.scalar.activation(v_sb[:].rearrange("p r h c -> p (r h c)"), p_m[:], ACT.Relu).then_inc(v_ready, 1)
                if slot == K_OUT:
                    if begun(g):
                        act.wait_ge(k_placed, 16 * 2 * S * PARTS * g)
                    act.wait_ge(k_made, g + 1)
                    nc.scalar.activation(k_hi[:], p_t[:].rearrange("p (r b k) -> p b r k", b=2, k=SEQ),
                                         ACT.Relu).then_inc(k_hi_ready, 1)
                if slot == Q_OUT:
                    if begun(g):
                        act.wait_ge(q_placed, 16 * 2 * S * PARTS * g)
                    act.wait_ge(q_made, g + 1)
                    nc.scalar.activation(q_hi[:], p_t[:].rearrange("p (r b k) -> p b k r", b=2, k=SEQ),
                                         ACT.Relu).then_inc(q_hi_ready, 1)

            def back(g, odd, slot, beside):
                if slot == EXP:
                    for r in range(PAIRS):
                        act.wait_ge(shifted, PAIRS * g + r + 1)
                        nc.scalar.activation(probs[:, r, :, :], probs[:, r, :, :], ACT.Exp, scale=NORM).then_inc(exp_done, 1)
                if EXP + 3 <= slot < EXP + 1 + PAIRS:
                    r = slot - EXP - 1
                    act.wait_ge(turned, PAIRS * g + r + 1)
                    act.wait_ge(av_done, PAIRS * g + r)
                    nc.scalar.copy(probsT[:].rearrange("p t m -> p (t m)"),
                                   p_s[:].rearrange("p s m -> p (s m)")).then_inc(pT_ready, 1)
                if slot == TURN_X2:
                    act.wait_ge(x2_turned, g + 1)
                    nc.scalar.copy(x2_hi[:, odd, :], p_t[:]).then_inc(x2_hi_ready, 1)
            def spread_weight(g, e):
                act.wait_ge(wb_made, E * g + e + 1)
                if e or begun(g):
                    act.wait_ge(prod_ready, E * g + e)
                nc.scalar.copy(wb[:], p_y[:, (e + 1) % 2, :]).then_inc(wb_ready, 1)

            def experts(g, odd, slot):
                if slot % CH == 2:
                    if slot > CH:
                        spread_weight(g, slot // CH - 1)
                    elif begun(g):
                        spread_weight(g - 1, E - 1)
                if slot == W_TURN + 1:
                    act.wait_ge(wT_turned, g + 1)
                    nc.scalar.copy(wT[0:2 * E, :], p_m[0:2 * E, :]).then_inc(wT_ready, 1)
                act.wait_ge(up_done, U * g + slot + 1)
                if slot >= NH or begun(g):
                    low_done(act, g, slot - NH)
                nc.scalar.activation(h_full[:, slot % NH, :], p_u[:, slot % 2, :], ACT.Gelu_apprx_tanh).then_inc(h_full_ready, 1)
                if slot % 2 == 0:
                    if slot >= NH or begun(g):
                        act.wait_ge(down_done, U * g + slot - NH + 1)
                    nc.scalar.activation(h_hi[:, slot % NH, :], p_u[:, slot % 2, :], ACT.Gelu_apprx_tanh).then_inc(h_hi_ready, 1)

            def drain(g):
                spread_weight(g - 1, E - 1)

            by_group(act, front, back, experts, drain)

        @block.vector
        def _(dve):
            nc.vector.memset(f32(q_rows[:]), 0.0).then_inc(zeroed, 1)
            nc.vector.memset(v_rows[:], 0.0).then_inc(zeroed, 1)
            nc.vector.memset(f32(wT[:]), 0.0).then_inc(zeroed, 1)
            nc.vector.memset(f32(k_rows[:]), 0.0).then_inc(zeroed, 1)
            dve.wait_ge(zeroed, 4)
            for hp in range(2):
                for r in range(PAIRS):
                    nc.vector.memset(v_rows[64 * hp:64 * hp + 64, r, :, hp, DH * T:], 1.0).then_inc(const_step, 1)
            dve.wait_ge(pool_const, 8)
            nc.vector.tensor_copy(pick[:].rearrange("p e m -> p (e m)"),
                                  probs[:, 0, :, :].rearrange("p h k -> p (h k)")).then_inc(pick_ready, 1)
            dve.wait_ge(w_turned, 1)
            for i in range(3):
                w = p_m[:, i * D:(i + 1) * D]
                w = w.rearrange("p (t h d) -> p h d t", h=2, d=DH) if i == 1 else w.rearrange("p (j s d) -> p s d j", s=S, d=DH)
                to = lambda t: t[:, i, :].rearrange("p (a b c) -> p a b c", a=2, b=DH)
                nc.vector.tensor_copy(to(w_hi), w).then_inc(w_step, 1)
                dve.wait_ge(w_step, i + 1)
                nc.vector.tensor_tensor(to(w_lo), w, f32(to(w_hi)), ALU.subtract).then_inc(w_split_done, 1)
            nc.vector.tensor_copy(r_hi[:], r_raw[:]).then_inc(w_step, 1)
            dve.wait_ge(w_step, 4)
            nc.vector.tensor_tensor(r_lo[:], r_raw[:], f32(r_hi[:]), ALU.subtract).then_inc(w_split_done, 1)
            def split_weights():
                raw = raw_weights()
                for loaded, hi, lo, done in ((up_loaded, up_hi[:].rearrange("p e h -> p (e h)"), up_lo[:].rearrange("p e h -> p (e h)"), up_split),
                                             (dn_loaded, dn_hi[:].rearrange("p e c d -> p (e c d)"), dn_lo[:].rearrange("p e c d -> p (e c d)"), dn_split)):
                    dve.wait_ge(loaded, 16)
                    nc.vector.tensor_copy(hi, raw).then_inc(done, 1)
                    dve.wait_ge(done, 1)
                    nc.vector.tensor_tensor(lo, raw, f32(hi), ALU.subtract).then_inc(done, 1)
                dve.wait_ge(dn_split, 2)

            def moments(g, k, src):
                for r in range(PAIRS):
                    i = nc.vector.bn_stats(stats[:, r, :], src[:, r, :])
                i.then_inc(ln_step[k], 1)
                dve.wait_ge(ln_step[k], 2 * g + 1)
                nc.vector.memset(var_eps[:], 0.0)
                for r in range(PAIRS):
                    i = nc.vector.bn_aggr(mean_var[:, r, :], stats[:, r, :])
                i.then_inc(ln_step[k], 1)
                dve.wait_ge(ln_step[k], 2 * g + 2)
                nc.vector.tensor_scalar(var_eps[:], mean_var[:, :, 1], EPS, None, ALU.add).then_inc(var_ready[k], 1)

            def normalise(g, k, src):
                dve.wait_ge(rstd_ready[k], g + 1)
                for r in range(PAIRS):
                    i = nc.vector.tensor_scalar(xn[:, r, :], src[:, r, :], mean_var[:, r, 0:1], rstd[:, r:r + 1],
                                                ALU.subtract, ALU.mult)
                i.then_inc(xn_ready[k], 1)

            def front(g, odd, slot):
                if slot == NORM1:
                    dve.wait_ge(x_loaded, 16 * (g + 1))
                    moments(g, 0, x_in[:, odd])
                if slot == NORM1 + 3:
                    if begun(g, 2):
                        dve.wait_ge(x2_turned, g - 1)
                    normalise(g, 0, x_in[:, odd])
                if slot == TURN_C:
                    dve.wait_ge(cT_hi_ready, g + 1)
                    nc.vector.tensor_tensor(cT_lo[:], p_t[:], f32(cT_hi[:]), ALU.subtract).then_inc(cT_lo_ready, 1)
                if slot == TURN_X:
                    dve.wait_ge(xT_hi_ready, g + 1)
                    nc.vector.tensor_tensor(xT_lo[:], p_t[:], f32(xT_hi[:]), ALU.subtract).then_inc(xT_lo_ready, 1)
                if slot == K_OUT:
                    dve.wait_ge(k_hi_ready, g + 1)
                    for b in range(2):
                        i = nc.vector.scalar_tensor_tensor(
                            out=k_lo[:, b, :, :], in0=p_t[:].rearrange("p (r b k) -> p b r k", b=2, k=SEQ)[:, b, :, :],
                            scalar=0.0, in1=f32(k_hi[:, b, :, :]), op0=ALU.max, op1=ALU.subtract)
                    i.then_inc(k_lo_ready, 1)
                if slot == Q_OUT:
                    dve.wait_ge(q_hi_ready, g + 1)
                    nc.vector.scalar_tensor_tensor(
                        out=q_lo[:].rearrange("p b k r -> p (b k) r"), in0=p_t[:].rearrange("p (r m) -> p m r", r=PAIRS),
                        scalar=0.0, in1=f32(q_hi[:]).rearrange("p b k r -> p (b k) r"), op0=ALU.max,
                        op1=ALU.subtract).then_inc(q_lo_ready, 1)
                if slot == U - 1 and not begun(g):
                    split_weights()

            def back(g, odd, slot, beside):
                if slot < EXP and slot % SCORE_EVERY < 2:
                    r = slot // SCORE_EVERY
                    sc = p_s[:].rearrange("p s (j k) -> p (s j) k", k=SEQ)
                    if slot % SCORE_EVERY == 0:
                        dve.wait_ge(scores_ready, PAIRS * g + r + 1)
                        nc.vector.tensor_reduce(row_max[:], sc, AX.X, ALU.max).then_inc(max_ready, 1)
                    else:
                        dve.wait_ge(max_ready, PAIRS * g + r + 1)
                        nc.vector.tensor_tensor(probs[:, r, :, :], sc, row_max[:].unsqueeze(2).broadcast_to([P, HEADS, SEQ]),
                                                ALU.subtract).then_inc(shifted, 1)
                if slot == EXP:
                    for r in range(2):
                        dve.wait_ge(turned, PAIRS * g + r + 1)
                        if r or begun(g):
                            dve.wait_ge(av_done, PAIRS * g + r)
                        nc.vector.tensor_copy(probsT[:].rearrange("p t m -> p (t m)"),
                                              p_s[:].rearrange("p s m -> p (s m)")).then_inc(pT_ready, 1)
                if slot == EXP or EXP + 2 < slot < EXP + 2 + PAIRS:
                    r = max(slot - EXP - 2, 0)
                    dve.wait_ge(av_done, PAIRS * g + r + 1)
                    o = p_m[:, 0:T * 4 * (DH + 1)].rearrange("p (t b h d) -> p b t h d", t=T, b=2, h=2)
                    inv = inv_sum[:].rearrange("p (t h) -> p t h", h=2)
                    for b in range(2):
                        rows = slice(64 * b, 64 * b + 64)
                        i = nc.vector.reciprocal(inv[rows], o[rows, b, :, :, DH])
                    i.then_inc(sums_ready, 1)
                    dve.wait_ge(sums_ready, PAIRS * g + r + 1)
                    for b in range(2):
                        rows = slice(64 * b, 64 * b + 64)
                        i = nc.vector.tensor_tensor(att[rows].rearrange("p (t h) d -> p t h d", h=2), o[rows, b, :, :, 0:DH],
                                                    inv[rows].unsqueeze(3).broadcast_to([64, T, 2, DH]), ALU.mult)
                    i.then_inc(o_read, 1)
                    dve.wait_ge(o_read, PAIRS * g + r + 1)
                    nc.vector.tensor_tensor(x1[:, odd, r, :], x_in[:, odd, r, :], att[:].rearrange("p h d -> p (h d)"),
                                            ALU.add).then_inc(x1_ready, 1)
                if slot == NORM2:
                    dve.wait_ge(x1_ready, PAIRS * (g + 1))
                    moments(g, 1, x1[:, odd])
                if slot == NORM2 + 1:
                    dve.wait_ge(x_turned, g + 1 + beside)
                    normalise(g, 1, x1[:, odd])
                if slot == TURN_X2:
                    dve.wait_ge(x2_hi_ready, g + 1)
                    nc.vector.tensor_tensor(x2_lo[:, odd, :], p_t[:], f32(x2_hi[:, odd, :]), ALU.subtract).then_inc(x2_lo_ready, 1)
                if slot == ROUTE + 1:
                    dve.wait_ge(logits_ready, g + 1)
                    lg = p_m[:, 0:PAIRS * E].rearrange("p (r e) -> p r e", e=E)
                    nc.vector.tensor_reduce(logit_max[:], lg, AX.X, ALU.max).then_inc(route_step, 1)
                    dve.wait_ge(route_step, 6 * g + 1)
                    nc.vector.tensor_tensor(logits[:], lg, logit_max[:].unsqueeze(2).broadcast_to([P, PAIRS, E]),
                                            ALU.subtract).then_inc(logits_read, 1)
                if slot == ROUTE + 2:
                    dve.wait_ge(logits_read, g + 1)
                    other = logits[:].unsqueeze(2).broadcast_to([P, PAIRS, E, E])
                    own = logits[:].unsqueeze(3).broadcast_to([P, PAIRS, E, E])
                    nc.vector.tensor_tensor(above[:], other, own, ALU.is_gt)
                    nc.vector.tensor_tensor(same[:], other, own, ALU.is_equal).then_inc(compared, 1)
                if slot == ROUTE + 5:
                    dve.wait_ge(rank_in, g + 1)
                    nc.vector.tensor_reduce(rank[:], above[:], AX.X, ALU.add).then_inc(route_step, 1)
                if slot == ROUTE + 7:
                    dve.wait_ge(powers, PAIRS * (g + 1))
                    dve.wait_ge(route_step, 6 * g + 2)
                    nc.vector.scalar_tensor_tensor(out=w_sel[:].rearrange("p r e -> p (r e)"), in0=rank[:].rearrange("p r e -> p (r e)"),
                                                   scalar=TOPK - 0.5, in1=expert_p[:].rearrange("p r e -> p (r e)"),
                                                   op0=ALU.is_lt, op1=ALU.mult).then_inc(route_step, 1)
                    dve.wait_ge(route_step, 6 * g + 3)
                    nc.vector.tensor_reduce(w_sum[:], w_sel[:], AX.X, ALU.add).then_inc(route_step, 1)
                if slot == ROUTE + 8:
                    dve.wait_ge(route_step, 6 * g + 4)
                    nc.vector.reciprocal(w_inv[:], w_sum[:]).then_inc(route_step, 1)
                    dve.wait_ge(route_step, 6 * g + 5)
                    nc.vector.tensor_tensor(w_norm[:], w_sel[:], w_inv[:].unsqueeze(2).broadcast_to([P, PAIRS, E]),
                                            ALU.mult).then_inc(route_step, 1)
                    dve.wait_ge(route_step, 6 * g + 6)
                    nc.vector.tensor_copy(w_round[:], w_norm[:]).then_inc(round_done, 1)
                    dve.wait_ge(round_done, g + 1)
                    nc.vector.tensor_copy(w_split[:, :, 0, :], f32(w_round[:]))
                    nc.vector.tensor_tensor(w_split[:, :, 1, :], w_norm[:], f32(w_round[:]), ALU.subtract).then_inc(weights_ready, 1)

            def weigh(g, odd, e):
                dve.wait_ge(down_done, U * g + CH * (e + 1))
                dve.wait_ge(wb_ready, E * g + e + 1)
                if e >= 3:
                    dve.wait_ge(acc_ready, (E - 1) * g + e - 2)
                elif e in (1, 2) and begun(g):
                    dve.wait_ge(acc_ready, (E - 1) * g)
                to = acc[:] if e == 0 else prod[:, e % 2, :]
                nc.vector.tensor_tensor(to, p_y[:, e % 2, :], wb[:], ALU.mult).then_inc(prod_ready, 1)

            def residual(g, odd):
                dve.wait_ge(out_turned, g + 1)
                if begun(g):
                    dve.wait_ge(stored, 16 * g)
                nc.vector.tensor_tensor(o_sb[:].rearrange("p r d -> p (r d)"), p_t[:],
                                        x1[:, odd].rearrange("p r d -> p (r d)"), ALU.add).then_inc(out_ready, 1)

            def experts(g, odd, slot):
                first = not begun(g)
                if slot % CH == 3:
                    if slot > CH:
                        weigh(g, odd, slot // CH - 1)
                    elif not first:
                        weigh(g - 1, 1 - odd, E - 1)
                dve.wait_ge(h_full_ready, U * g + slot + 1)
                if slot % 2:
                    if slot >= NH or not first:
                        dve.wait_ge(down_done, U * g + slot - NH + 1)
                    nc.vector.tensor_copy(h_hi[:, slot % NH, :], h_full[:, slot % NH, :]).then_inc(h_hi_dve, 1)
                if slot in DVE_LOW:
                    if slot % 2:
                        dve.wait_ge(h_hi_dve, U // 2 * g + slot // 2 + 1)
                    else:
                        dve.wait_ge(h_hi_ready, U // 2 * g + slot // 2 + 1)
                    nc.vector.tensor_tensor(h_lo[:, slot % NH, :], h_full[:, slot % NH, :], f32(h_hi[:, slot % NH, :]),
                                            ALU.subtract).then_inc(h_lo_ready, 1)
                if slot == OUT and not first:
                    residual(g - 1, 1 - odd)

            def drain(g):
                weigh(g - 1, 1, E - 1)
                residual(g - 1, 1)

            by_group(dve, front, back, experts, drain)

        @block.tensor
        def _(pe):
            pe.wait_ge(w_loaded, 64)
            pe.wait_ge(pool_const, 5)
            for i in range(3):
                mm = nc.tensor.transpose(p_m[:, i * D:(i + 1) * D], w_raw[:, i, :], ident[:])
            mm.then_inc(w_turned, 1)
            pe.wait_ge(w_split_done, 4)

            def three(out, lhs_hi, lhs_lo, rhs_hi, rhs_lo, start=True, stop=True):
                nc.tensor.matmul(out, lhs_hi, rhs_hi, start=start, stop=False)
                nc.tensor.matmul(out, lhs_hi, rhs_lo, start=False, stop=False)
                return nc.tensor.matmul(out, lhs_lo, rhs_hi, start=False, stop=stop)

            def turn(bank, src):
                for r in range(4):
                    mm = nc.tensor.transpose(bank[:, r * P:(r + 1) * P], src[:, r, :], ident[:])
                return mm

            def front(g, odd, slot):
                if slot == TURN_C:
                    pe.wait_ge(c_loaded, 16 * (g + 1))
                    if begun(g, 2):
                        pe.wait_ge(x2_hi_ready, g - 1)
                        pe.wait_ge(x2_lo_ready, g - 1)
                    turn(p_t, c_in).then_inc(c_turned, 1)
                if slot == TURN_X:
                    pe.wait_ge(xn_ready[0], g + 1)
                    if begun(g, 3):
                        pe.wait_ge(out_ready, g - 2)
                    turn(p_t, xn).then_inc(x_turned, 1)
                if slot == V_OUT:
                    pe.wait_ge(cT_hi_ready, g + 1)
                    pe.wait_ge(cT_lo_ready, g + 1)
                    if begun(g, 2):
                        pe.wait_ge(wT_ready, g - 1)
                    for r in range(PAIRS):
                        tok = slice(r * P, (r + 1) * P)
                        mm = three(p_m[:, tok], cT_hi[:, tok], cT_lo[:, tok], w_hi[:, 1, :], w_lo[:, 1, :])
                    mm.then_inc(v_made, 1)
                if slot == K_OUT:
                    pe.wait_ge(xT_hi_ready, g + 1)
                    pe.wait_ge(xT_lo_ready, g + 1)
                    three(p_t[:], w_hi[:, 0, :], w_lo[:, 0, :], cT_hi[:], cT_lo[:]).then_inc(k_made, 1)
                if slot == Q_OUT:
                    pe.wait_ge(k_hi_ready, g + 1)
                    pe.wait_ge(k_lo_ready, g + 1)
                    three(p_t[:], w_hi[:, 2, :], w_lo[:, 2, :], xT_hi[:], xT_lo[:]).then_inc(q_made, 1)

            def back(g, odd, slot, beside):
                if slot < EXP and slot % SCORE_EVERY == 0:
                    r = slot // SCORE_EVERY
                    if r == 0:
                        if begun(g):
                            pe.wait_ge(pT_ready, PAIRS * g)
                        pe.wait_ge(k_placed, 16 * 2 * S * PARTS * (g + 1))
                        pe.wait_ge(q_placed, 16 * 2 * S * PARTS * (g + 1))
                    else:
                        pe.wait_ge(shifted, PAIRS * g + r)
                    for j in range(J):
                        mm = nc.tensor.matmul(p_s[:, j // 4, j % 4 * S * SEQ:(j % 4 + 1) * S * SEQ], q_rows[:, j, :, r],
                                              k_rows[:, j, :, r, :], start=True, stop=True)
                    mm.then_inc(scores_ready, 1)
                if EXP + 2 <= slot < EXP + 2 + PAIRS:
                    r = slot - EXP - 2
                    pe.wait_ge(pT_ready, PAIRS * g + r + 1)
                    if r == 0:
                        pe.wait_ge(v_placed, 16 * 4 * (g + 1))
                        if beside:
                            pe.wait_ge(v_ready, g + 2)
                    else:
                        pe.wait_ge(o_read, PAIRS * g + r)
                    vr = v_rows[:, r, :, :, :].rearrange("p b h (d t) -> p (b h) d t", t=T)
                    w = 4 * (DH + 1)
                    for t in range(T):
                        mm = nc.tensor.matmul(p_m[:, t * w:(t + 1) * w], probsT[:, t, :], vr[:, :, :, t], start=True, stop=True)
                    mm.then_inc(av_done, 1)
                if EXP + 1 <= slot < EXP + 1 + PAIRS:
                    r = slot - EXP - 1
                    if r == 0:
                        pe.wait_ge(shifted, PAIRS * (g + 1))
                    pe.wait_ge(exp_done, PAIRS * g + r + 1)
                    for t in range(T):
                        mm = nc.tensor.transpose(p_s[:, t // 4, t % 4 * P:(t % 4 + 1) * P],
                                                 probs[:, r, 2 * t:2 * t + 2, :].rearrange("p h k -> p (h k)"), ident[:])
                    mm.then_inc(turned, 1)
                if slot == TURN_X2:
                    pe.wait_ge(xn_ready[1], g + 1)
                    if beside:
                        pe.wait_ge(q_hi_ready, g + 2)
                        pe.wait_ge(q_lo_ready, g + 2)
                    turn(p_t, xn).then_inc(x2_turned, 1)
                if slot == ROUTE:
                    pe.wait_ge(x2_hi_ready, g + 1)
                    pe.wait_ge(x2_lo_ready, g + 1)
                    pe.wait_ge(o_read, PAIRS * (g + 1))
                    for r in range(PAIRS):
                        tok = slice(r * P, (r + 1) * P)
                        mm = three(p_m[:, r * E:(r + 1) * E], x2_hi[:, odd, tok], x2_lo[:, odd, tok], r_hi[:], r_lo[:])
                    mm.then_inc(logits_ready, 1)
            def down(g, unit):
                e, c = unit // CH, unit % CH
                if unit % 2:
                    pe.wait_ge(h_hi_dve, U // 2 * g + unit // 2 + 1)
                else:
                    pe.wait_ge(h_hi_ready, U // 2 * g + unit // 2 + 1)
                low_done(pe, g, unit)
                if c == 0 and (e or begun(g)):
                    pe.wait_ge(wb_ready, E * g + e)
                three(p_y[:, e % 2, :], dn_hi[:, e, c, :], dn_lo[:, e, c, :], h_hi[:, unit % NH, :], h_lo[:, unit % NH, :],
                      start=(c == 0), stop=(c == CH - 1)).then_inc(down_done, 1)

            def turn_out(g, odd):
                pe.wait_ge(acc_ready, (E - 1) * (g + 1))
                turn(p_t, acc[:].rearrange("p (r m) -> p r m", r=PAIRS)).then_inc(out_turned, 1)

            def spread_weight(g, odd, e):
                if e == 0:
                    pe.wait_ge(wT_ready, g + 1)
                if e or begun(g):
                    pe.wait_ge(prod_ready, E * g + e)
                nc.tensor.matmul(p_y[:, (e + 1) % 2, :], pick[:, e, :], wT[:], start=True, stop=True).then_inc(wb_made, 1)

            def experts(g, odd, slot):
                first = not begun(g)
                e, c = slot // CH, slot % CH
                if slot == 0:
                    pe.wait_ge(x2_lo_ready, g + 1)
                    pe.wait_ge(x2_hi_ready, g + 1)
                    if first:
                        pe.wait_ge(dn_split, 2)
                if slot >= 2 or not first:
                    if slot % 2:
                        pe.wait_ge(h_full_ready, U * g + slot - 1)
                    else:
                        pe.wait_ge(h_hi_ready, U // 2 * g + slot // 2)
                hid = slice(c * P, (c + 1) * P)
                three(p_u[:, slot % 2, :], up_hi[:, e, hid], up_lo[:, e, hid], x2_hi[:, odd, :], x2_lo[:, odd, :]).then_inc(up_done, 1)
                if slot >= LAG:
                    down(g, slot - LAG)
                elif not first:
                    down(g - 1, U + slot - LAG)
                if c == 1:
                    if e:
                        spread_weight(g, odd, e - 1)
                    elif not first:
                        spread_weight(g - 1, 1 - odd, E - 1)
                if slot == W_TURN:
                    pe.wait_ge(weights_ready, g + 1)
                    for r in range(PAIRS):
                        mm = nc.tensor.transpose(p_m[0:2 * E, r * P:(r + 1) * P],
                                                 w_split[:, r, :, :].rearrange("p a e -> p (a e)"), ident[:])
                    mm.then_inc(wT_turned, 1)
                if slot == OUT and not first:
                    turn_out(g - 1, 1 - odd)

            def drain(g):
                for unit in range(U - LAG, U):
                    down(g - 1, unit)
                    if unit == U - 2:
                        spread_weight(g - 1, 1, E - 1)
                turn_out(g - 1, 1)

            by_group(pe, front, back, experts, drain)


_INS = ['x', 'ctx_1024', 'L0_xattn_Wq', 'L0_xattn_Wk', 'L0_xattn_Wv', 'L0_ffn_router_w', 'L0_ffn_up_w', 'L0_ffn_down_w']
_OUTS = [((128, 64, 128), 'float32')]


def kernel(**inputs):
    import numpy as _np
    import concourse.bacc as _bacc
    from concourse import mybir as _mybir
    from concourse.bass_utils import run_bass_kernel_spmd as _run

    nc = _bacc.Bacc("TRN2", target_bir_lowering=False, num_devices=1)
    arrays, args = {}, []
    for name in _INS:
        a = _np.ascontiguousarray(inputs[name])
        arrays[f"in_{name}_dram"] = a
        args.append(nc.dram_tensor(f"in_{name}_dram", a.shape, _mybir.dt.from_np(a.dtype), kind="ExternalInput").ap())
    for i, (shape, dtype) in enumerate(_OUTS):
        dt = _mybir.dt.from_np(_np.dtype(dtype))
        args.append(nc.dram_tensor(f"out_{i}_dram", shape, dt, kind="ExternalOutput").ap())
    build(nc, *args)
    r = _run(nc, [arrays], core_ids=[0])
    return r.results[0]["out_0_dram"]
```

```python
from contextlib import ExitStack

import concourse.bass as bass
from concourse import mybir

F32 = mybir.dt.float32
F32R = mybir.dt.float32r
ALU = mybir.AluOpType
ACT = mybir.ActivationFunctionType
AX = mybir.AxisListType

P = 128
HEADS = 16
TOPK = 4
EPS = 1e-5
E_BASE = 2.718281828459045


def build(nc, x, ctx_in, wq, wk, wv, router_w, up_w, down_w, out):
    NSEQ, SEQ, D = x.shape
    _, _, HID = up_w.shape
    E = router_w.shape[1]
    DH = D // HEADS
    NORM = float(DH) ** -0.5
    PAIR = 2 * SEQ
    TOK = 512
    PAIRS = TOK // PAIR
    G = NSEQ * SEQ // TOK
    S = 2
    J = HEADS // S
    PARTS = 4
    SPREAD = 16 * 2 * PARTS
    T = HEADS // 2
    CH = HID // P
    U = E * CH
    LAG = 3
    TURN_C, NORM1, TURN_X, K_OUT, Q_OUT, V_OUT, V_MOVE = 2, 4, 7, 10, 12, 14, 18
    SCORE_EVERY = 3
    EXP = SCORE_EVERY * PAIRS
    NORM2, TURN_X2, ROUTE = 18, 22, 24
    POWERS = (25, 26, 27, 29)
    W_TURN, OUT = 2, EXP
    NH = 4
    ACT_HI = [slot for slot in range(0, U, 2) if slot != EXP]
    DVE_HI = [slot for slot in range(U) if slot not in ACT_HI]
    POOL_LOW = [slot for slot in range(U) if (slot % 2 and slot < POWERS[0] and slot != 19) or slot in (0, 2, 4, 6, 10)]
    DVE_LOW = [slot for slot in range(U) if slot not in POOL_LOW]
    assert PAIR == P and D == P and S * 2 * PARTS * DH == P and G % 2 == 0

    x_v = x.rearrange("(g r b) s d -> g (b s) r d", r=PAIRS, b=2)
    c_v = ctx_in.rearrange("(g r b) s d -> g (b s) r d", r=PAIRS, b=2)
    o_v = out.rearrange("(g r b) s d -> g (b s) r d", r=PAIRS, b=2)

    with ExitStack() as stack:
        def sb(name, shape, dt=F32):
            return stack.enter_context(nc.sbuf_tensor(name, shape, dt))

        def ps(name, shape):
            return stack.enter_context(nc.psum_tensor(name, shape, F32))

        def sem(name):
            return stack.enter_context(nc.semaphore(name))

        up_hi = sb("up_hi", [P, E, HID], F32R)
        up_lo = sb("up_lo", [P, E, HID], F32R)
        dn_hi = sb("dn_hi", [P, E, CH, D], F32R)
        dn_lo = sb("dn_lo", [P, E, CH, D], F32R)
        w_hi = sb("w_hi", [P, 3, D], F32R)
        w_lo = sb("w_lo", [P, 3, D], F32R)
        r_raw = sb("r_raw", [P, E])
        r_both = sb("r_both", [P, 2, E], F32R)
        ident = sb("ident", [P, P])
        pick = sb("pick", [P, E, P], F32R)
        earlier = sb("earlier", [P, E, E])
        minus_half = sb("minus_half", [P, PAIRS])
        e_base = sb("e_base", [P, E])
        x_in = sb("x_in", [P, 2, PAIRS, D])
        c_in = sb("c_in", [P, PAIRS, D])
        o_sb = c_in
        stats = sb("stats", [P, PAIRS, 6])
        mean_var = sb("mean_var", [P, PAIRS, 2])
        var_eps = sb("var_eps", [P, PAIRS])
        rstd = sb("rstd", [P, PAIRS])
        xn = sb("xn", [P, PAIRS, D])
        cT_hi = sb("cT_hi", [P, TOK], F32R)
        cT_lo = sb("cT_lo", [P, TOK], F32R)
        xT_hi = sb("xT_hi", [P, TOK], F32R)
        xT_lo = sb("xT_lo", [P, TOK], F32R)
        q_hi = sb("q_hi", [P, 2, SEQ, PAIRS], F32R)
        q_lo = sb("q_lo", [P, 2, SEQ, PAIRS], F32R)
        k_hi = sb("k_hi", [P, 2, PAIRS, SEQ], F32R)
        k_lo = sb("k_lo", [P, 2, PAIRS, SEQ], F32R)
        v_sb = sb("v_sb", [P, PAIRS, 2, DH * T])
        q_rows = sb("q_rows", [P, J, 2 * SEQ, PAIRS], F32R)
        k_rows = sb("k_rows", [P, J, S, PAIRS, SEQ], F32R)
        v_rows = sb("v_rows", [P, PAIRS, 2, 2, (DH + 1) * T])
        row_max = sb("row_max", [P, 2, HEADS])
        probs = sb("probs", [P, PAIRS, HEADS, SEQ])
        probsT = sb("probsT", [P, 2, T, P])
        inv_sum = sb("inv_sum", [P, HEADS])
        att = sb("att", [P, 2, HEADS, DH])
        x1 = sb("x1", [P, 2, PAIRS, D])
        x2_hi = sb("x2_hi", [P, 2, TOK], F32R)
        x2_lo = sb("x2_lo", [P, 2, TOK], F32R)
        wT = sb("wT", [P, TOK], F32R)
        logit_max = sb("logit_max", [P, PAIRS])
        logits = sb("logits", [P, PAIRS, E])
        logits_low = sb("logits_low", [P, PAIRS, E])
        expert_p = sb("expert_p", [P, PAIRS, E])
        compares = xn[:].rearrange("p r d -> p (r d)").rearrange("p (k r e f) -> p k r e f", k=2, r=PAIRS, e=E)
        above, same = compares[:, 0], compares[:, 1]
        rank = sb("rank", [P, PAIRS, E])
        w_sel = sb("w_sel", [P, PAIRS, E])
        w_sum = sb("w_sum", [P, PAIRS])
        w_inv = sb("w_inv", [P, PAIRS])
        w_norm = sb("w_norm", [P, PAIRS, E])
        w_round = sb("w_round", [P, PAIRS, E], F32R)
        w_split = sb("w_split", [P, PAIRS, 2, E])
        h_full = sb("h_full", [P, NH, TOK])
        w_raw = h_full[:].rearrange("p a m -> p (a m)")[:, 0:3 * D].rearrange("p (i d) -> p i d", i=3)
        h_hi = sb("h_hi", [P, NH, TOK], F32R)
        h_lo = sb("h_lo", [P, NH, TOK], F32R)
        wb = sb("wb", [P, TOK])
        prod = sb("prod", [P, 2, TOK])
        acc = sb("acc", [P, TOK])

        p_s = ps("p_s", [P, 2, 512])
        p_t = ps("p_t", [P, 512])
        p_m = ps("p_m", [P, 512])
        p_u = ps("p_u", [P, 2, 512])
        p_y = ps("p_y", [P, 2, 512])

        up_loaded = sem("up_loaded")
        dn_loaded = sem("dn_loaded")
        w_loaded = sem("w_loaded")
        x_loaded = sem("x_loaded")
        c_loaded = sem("c_loaded")
        q_placed = sem("q_placed")
        q_placed_by_pool = sem("q_placed_by_pool")
        k_placed = sem("k_placed")
        v_placed = sem("v_placed")
        stored = sem("stored")
        pool_const = sem("pool_const")
        zeroed = sem("zeroed")
        k_zeroed = sem("k_zeroed")
        v_zeroed = sem("v_zeroed")
        w_turned = sem("w_turned")
        w_step = sem("w_step")
        up_hi_ready = sem("up_hi_ready")
        dn_hi_ready = sem("dn_hi_ready")
        up_split = sem("up_split")
        dn_split = sem("dn_split")
        w_split_done = sem("w_split_done")
        pick_ready = sem("pick_ready")
        var_ready = [sem(f"var_ready_{k}") for k in (1, 2)]
        rstd_ready = [sem(f"rstd_ready_{k}") for k in (1, 2)]
        ln_step = [sem(f"ln_step_{k}") for k in (1, 2)]
        xn_ready = [sem(f"xn_ready_{k}") for k in (1, 2)]
        c_turned = sem("c_turned")
        x_turned = sem("x_turned")
        cT_hi_ready = sem("cT_hi_ready")
        cT_lo_ready = sem("cT_lo_ready")
        xT_hi_ready = sem("xT_hi_ready")
        xT_lo_ready = sem("xT_lo_ready")
        k_made = sem("k_made")
        v_made = sem("v_made")
        q_made = sem("q_made")
        k_hi_ready = sem("k_hi_ready")
        k_lo_ready = sem("k_lo_ready")
        v_ready = sem("v_ready")
        q_hi_ready = sem("q_hi_ready")
        q_lo_ready = sem("q_lo_ready")
        scores_ready = sem("scores_ready")
        max_ready = sem("max_ready")
        shifted = sem("shifted")
        exp_done = sem("exp_done")
        turned = sem("turned")
        pT_ready = sem("pT_ready")
        av_done = sem("av_done")
        sums_ready = sem("sums_ready")
        o_read = sem("o_read")
        x1_ready = sem("x1_ready")
        x2_turned = sem("x2_turned")
        x2_hi_ready = sem("x2_hi_ready")
        x2_lo_ready = sem("x2_lo_ready")
        logits_ready = sem("logits_ready")
        route_step = sem("route_step")
        logits_summed = sem("logits_summed")
        logits_read = sem("logits_read")
        powers = sem("powers")
        ties_marked = sem("ties_marked")
        rank_in = sem("rank_in")
        weights_ready = sem("weights_ready")
        wT_turned = sem("wT_turned")
        round_done = sem("round_done")
        compared = sem("compared")
        wT_ready = sem("wT_ready")
        wb_made = sem("wb_made")
        wb_ready = sem("wb_ready")
        up_done = sem("up_done")
        h_full_ready = sem("h_full_ready")
        h_hi_act = sem("h_hi_act")
        h_hi_dve = sem("h_hi_dve")
        h_lo_dve = sem("h_lo_dve")
        h_lo_pool = sem("h_lo_pool")
        down_done = sem("down_done")
        prod_ready = sem("prod_ready")
        acc_ready = sem("acc_ready")
        out_turned = sem("out_turned")
        out_ready = sem("out_ready")

        block = stack.enter_context(nc.Block())

        def f32(ap):
            return ap.bitcast(F32)

        def raw_weights():
            return probs[:].rearrange("p r h k -> p (r h k)")

        def raw_pick():
            return h_full[:, 2:4, :].rearrange("p a m -> p (a m)")

        def raw_down():
            return (probsT[:, 0].rearrange("p t m -> p (t m)"), v_rows[:].rearrange("p r b h c -> p (r b h c)")[:, 0:2 * HID],
                    x1[:].rearrange("p a r d -> p (a r d)"), prod[:].rearrange("p a m -> p (a m)"))

        def by_group(eng, front, back, experts, drain):
            def step(g, odd, with_experts, with_back, with_front):
                for slot in range(U):
                    if with_experts:
                        experts(g, odd, slot)
                    if with_front:
                        front(g + 2, odd, slot)
                    if with_back:
                        back(g + 1, 1 - odd, slot, with_front)

            step(-2, 0, False, False, True)
            step(-1, 1, False, True, True)
            step(0, 0, True, True, True)
            with eng.Fori(0, (G - 4) // 2) as i:
                step(2 * i + 1, 1, True, True, True)
                step(2 * i + 2, 0, True, True, True)
            step(G - 3, 1, True, True, True)
            step(G - 2, 0, True, True, False)
            step(G - 1, 1, True, False, False)
            drain(G)

        def high_done(eng, g, slot):
            if slot < 0:
                g, slot = g - 1, slot + U
            if slot in ACT_HI:
                eng.wait_ge(h_hi_act, len(ACT_HI) * g + ACT_HI.index(slot) + 1)
            else:
                eng.wait_ge(h_hi_dve, len(DVE_HI) * g + DVE_HI.index(slot) + 1)

        def low_done(eng, g, slot):
            if slot < 0:
                g, slot = g - 1, slot + U
            if slot in POOL_LOW:
                eng.wait_ge(h_lo_pool, len(POOL_LOW) * g + POOL_LOW.index(slot) + 1)
            else:
                eng.wait_ge(h_lo_dve, len(DVE_LOW) * g + DVE_LOW.index(slot) + 1)

        def k_out(g):
            return K_OUT if begun(g) else TURN_C + 1

        def pair_bank(g, r):
            return p_u if r % 2 and not begun(g) else p_s

        def spread(eng, s, rows_of, placed):
            for b in range(2):
                for part in range(PARTS):
                    row = 2 * PARTS * DH * s + PARTS * DH * b + DH * part
                    to, src = rows_of(s, b, part, slice(row, row + DH))
                    eng.dma_start(f32(to), f32(src[J * DH * s:J * DH * (s + 1), b, :, :])).then_inc(placed, 16)

        def q_moves(n):
            return (S * n - 1) * SPREAD

        def k_rows_of(s, b, part, rows):
            return k_rows[rows, :, s, :, :], (k_hi, k_lo)[part % 2]

        def q_rows_of(s, b, part, rows):
            return q_rows[rows, :, SEQ * b:SEQ * b + SEQ, :], (q_hi, q_lo)[part // 2]

        def begun(g, n=1):
            return not isinstance(g, int) or g >= n

        @block.sync
        def _(sp):
            for i, w in enumerate((wk, wv, wq)):
                sp.dma_start(w_raw[:, i, :], w).then_inc(w_loaded, 16)
            sp.dma_start(r_raw[:], router_w).then_inc(w_loaded, 16)

            def load_x_c(g, odd):
                if begun(g, 4):
                    sp.wait_ge(stored, 16 * (g - 3))
                sp.dma_start(c_in[:], c_v[g]).then_inc(c_loaded, 16)
                if begun(g, 2):
                    sp.wait_ge(x1_ready, PAIRS * (g - 1))
                sp.dma_start(x_in[:, odd], x_v[g]).then_inc(x_loaded, 16)

            def front(g, odd, slot):
                if slot == 0 and not begun(g):
                    load_x_c(0, 0)
                    sp.dma_start(raw_weights().rearrange("p (e h) -> p e h", e=E),
                                 up_w.rearrange("e d h -> d e h")).then_inc(up_loaded, 16)
                    for i, raw in enumerate(raw_down()):
                        sp.dma_start(raw.rearrange("p (e c d) -> p e c d", e=2, c=CH),
                                     down_w[2 * i:2 * i + 2].rearrange("e (c p) d -> p e c d", p=P)).then_inc(dn_loaded, 16)
                if slot == k_out(g) + 1:
                    if not begun(g):
                        sp.wait_ge(k_zeroed, 1)
                    sp.wait_ge(k_hi_ready, g + 1)
                    sp.wait_ge(k_lo_ready, g + 1)
                    for s in range(S):
                        spread(sp, s, k_rows_of, k_placed)
                if slot == Q_OUT + 1:
                    sp.wait_ge(q_hi_ready, g + 1)
                    sp.wait_ge(q_lo_ready, g + 1)
                    spread(sp, 0, q_rows_of, q_placed)
                    if begun(g):
                        spread(sp, 1, q_rows_of, q_placed)
                if slot == V_MOVE:
                    if not (isinstance(g, int) and g == G - 1):
                        load_x_c(g + 1, 1 - odd)
                    if not begun(g):
                        sp.wait_ge(v_zeroed, 1 + 2 * PAIRS)
                    if begun(g):
                        sp.wait_ge(av_done, PAIRS * g)
                    sp.wait_ge(v_ready, g + 1)
                    for hp in range(2):
                        for b in range(2):
                            sp.dma_start(v_rows[SEQ * hp:SEQ * (hp + 1), :, b, hp, 0:DH * T],
                                         v_sb[SEQ * b:SEQ * (b + 1), :, hp, :]).then_inc(v_placed, 16)

            def back(g, odd, slot, beside):
                pass

            def store(g):
                sp.wait_ge(out_ready, g + 1)
                sp.dma_start(o_v[g], o_sb[:]).then_inc(stored, 16)

            def experts(g, odd, slot):
                if slot == OUT + 1 and begun(g):
                    store(g - 1)

            def drain(g):
                store(g - 1)
                sp.wait_ge(stored, 16 * G)

            by_group(sp, front, back, experts, drain)

        @block.gpsimd
        def _(pool):
            sel = raw_pick().rearrange("p (e m) -> p e m", e=E)
            nc.gpsimd.memset(ident[:], 0.0).then_inc(pool_const, 1)
            nc.gpsimd.memset(earlier[:], 1.0).then_inc(pool_const, 1)
            nc.gpsimd.memset(sel, 0.0).then_inc(pool_const, 1)
            nc.gpsimd.memset(minus_half[:], -0.5)
            nc.gpsimd.memset(e_base[:], E_BASE).then_inc(pool_const, 1)
            pool.wait_ge(pool_const, 4)
            nc.gpsimd.affine_select(out=ident[:], in_=ident[:], compare_op=ALU.not_equal, fill=1.0, base=0,
                                    pattern=[[-1, P]], channel_multiplier=1).then_inc(pool_const, 1)
            nc.gpsimd.affine_select(out=earlier[:], in_=earlier[:], compare_op=ALU.is_gt, fill=0.0, base=0,
                                    pattern=[[1, E], [-1, E]], channel_multiplier=0).then_inc(pool_const, 1)
            nc.gpsimd.affine_select(out=sel, in_=sel, compare_op=ALU.not_equal, fill=1.0, base=0,
                                    pattern=[[-1, E], [0, P]], channel_multiplier=1).then_inc(pool_const, 1)
            pool.wait_ge(pool_const, 7)
            nc.gpsimd.affine_select(out=sel, in_=sel, compare_op=ALU.not_equal, fill=1.0, base=-E,
                                    pattern=[[-1, E], [0, P]], channel_multiplier=1).then_inc(pool_const, 1)

            nc.gpsimd.memset(f32(k_rows[:]), 0.0).then_inc(k_zeroed, 1)

            def inv_root(g, k):
                pool.wait_ge(var_ready[k], g + 1)
                nc.gpsimd.tensor_tensor(rstd[:], var_eps[:], minus_half[:], ALU.pow).then_inc(rstd_ready[k], 1)

            def front(g, odd, slot):
                if slot == NORM1:
                    inv_root(g, 0)
                if slot == Q_OUT + 1 and not begun(g):
                    pool.wait_ge(q_hi_ready, 1)
                    pool.wait_ge(q_lo_ready, 1)
                    spread(nc.gpsimd, 1, q_rows_of, q_placed_by_pool)

            def back(g, odd, slot, beside):
                if slot == EXP + 1 or EXP + 2 < slot < EXP + 2 + PAIRS:
                    r = max(slot - EXP - 2, 0)
                    pool.wait_ge(o_read, PAIRS * g + r + 1)
                    nc.gpsimd.tensor_tensor(x1[:, odd, r, :], x_in[:, odd, r, :], att[:, r % 2].rearrange("p h d -> p (h d)"),
                                            ALU.add).then_inc(x1_ready, 1)
                if slot == NORM2:
                    inv_root(g, 1)
                if slot in POWERS:
                    r = POWERS.index(slot)
                    pool.wait_ge(logits_read, g + 1)
                    nc.gpsimd.tensor_tensor(expert_p[:, r, :], e_base[:], logits[:, r, :], ALU.pow).then_inc(powers, 1)

            def add(g, e):
                pool.wait_ge(prod_ready, E * g + e + 1)
                if e >= 2:
                    pool.wait_ge(acc_ready, (E - 1) * g + e - 1)
                elif begun(g):
                    pool.wait_ge(out_turned, g)
                nc.gpsimd.tensor_tensor(acc[:], acc[:] if e >= 2 else prod[:, 0, :], prod[:, e % 2, :], ALU.add).then_inc(acc_ready, 1)

            def experts(g, odd, slot):
                if slot in (0, CH) and begun(g):
                    add(g - 1, E - 2 + slot // CH)
                if slot % CH == 0 and slot // CH >= 3:
                    add(g, slot // CH - 2)
                if slot in POOL_LOW:
                    high_done(pool, g, slot)
                    nc.gpsimd.tensor_tensor(h_lo[:, slot % NH, :], h_full[:, slot % NH, :], f32(h_hi[:, slot % NH, :]),
                                            ALU.subtract).then_inc(h_lo_pool, 1)

            def drain(g):
                add(g - 1, E - 2)
                add(g - 1, E - 1)

            by_group(pool, front, back, experts, drain)

        @block.scalar
        def _(act):
            def front(g, odd, slot):
                if slot == TURN_C:
                    act.wait_ge(c_turned, g + 1)
                    nc.scalar.copy(cT_hi[:], p_t[:]).then_inc(cT_hi_ready, 1)
                if slot == TURN_X:
                    act.wait_ge(x_turned, g + 1)
                    nc.scalar.copy(xT_hi[:], p_t[:]).then_inc(xT_hi_ready, 1)
                if slot == k_out(g):
                    if begun(g):
                        act.wait_ge(k_placed, S * SPREAD * g)
                    act.wait_ge(k_made, g + 1)
                    nc.scalar.activation(k_hi[:], p_t[:].rearrange("p (r b k) -> p b r k", b=2, k=SEQ),
                                         ACT.Relu).then_inc(k_hi_ready, 1)
                if slot == Q_OUT and not begun(g):
                    act.wait_ge(up_loaded, 16)
                    nc.scalar.copy(up_hi[:].rearrange("p e h -> p (e h)"), raw_weights()).then_inc(up_hi_ready, 1)
                    act.wait_ge(dn_loaded, 64)
                    for i, raw in enumerate(raw_down()):
                        nc.scalar.copy(dn_hi[:, 2 * i:2 * i + 2].rearrange("p e c d -> p (e c d)"), raw).then_inc(dn_hi_ready, 1)
                if slot == V_OUT:
                    if begun(g):
                        act.wait_ge(v_placed, 16 * 4 * g)
                    act.wait_ge(v_made, g + 1)
                    nc.scalar.activation(v_sb[:].rearrange("p r h c -> p (r h c)"), p_t[:], ACT.Relu).then_inc(v_ready, 1)

            def back(g, odd, slot, beside):
                if slot == EXP:
                    for r in range(PAIRS):
                        act.wait_ge(shifted, PAIRS * g + r + 1)
                        nc.scalar.activation(probs[:, r, :, :], probs[:, r, :, :], ACT.Exp, scale=NORM).then_inc(exp_done, 1)
                if EXP + 3 <= slot < EXP + 1 + PAIRS:
                    r = slot - EXP - 1
                    act.wait_ge(turned, PAIRS * g + r + 1)
                    act.wait_ge(av_done, PAIRS * g + r - 1)
                    nc.scalar.copy(probsT[:, r % 2].rearrange("p t m -> p (t m)"),
                                   pair_bank(g, r)[:].rearrange("p s m -> p (s m)")).then_inc(pT_ready, 1)
                if slot == TURN_X2:
                    act.wait_ge(x2_turned, g + 1)
                    nc.scalar.copy(x2_hi[:, odd, :], p_t[:]).then_inc(x2_hi_ready, 1)

            def spread_weight(g, e):
                act.wait_ge(wb_made, E * g + e + 1)
                if e or begun(g):
                    act.wait_ge(prod_ready, E * g + e)
                nc.scalar.copy(wb[:], p_y[:, (e + 1) % 2, :]).then_inc(wb_ready, 1)

            def experts(g, odd, slot):
                if slot % CH == 2:
                    if slot > CH:
                        spread_weight(g, slot // CH - 1)
                    elif begun(g):
                        spread_weight(g - 1, E - 1)
                if slot == W_TURN + 1:
                    act.wait_ge(wT_turned, g + 1)
                    nc.scalar.copy(wT[0:2 * E, :], p_m[0:2 * E, :]).then_inc(wT_ready, 1)
                act.wait_ge(up_done, U * g + slot + 1)
                if slot >= NH or begun(g):
                    low_done(act, g, slot - NH)
                nc.scalar.activation(h_full[:, slot % NH, :], p_u[:, slot % 2, :], ACT.Gelu_apprx_tanh).then_inc(h_full_ready, 1)
                if slot in ACT_HI:
                    if slot >= NH or begun(g):
                        act.wait_ge(down_done, U * g + slot - NH + 1)
                    nc.scalar.activation(h_hi[:, slot % NH, :], p_u[:, slot % 2, :], ACT.Gelu_apprx_tanh).then_inc(h_hi_act, 1)

            def drain(g):
                spread_weight(g - 1, E - 1)

            by_group(act, front, back, experts, drain)

        @block.vector
        def _(dve):
            nc.vector.memset(f32(q_rows[:]), 0.0).then_inc(zeroed, 1)
            dve.wait_ge(w_turned, 1)
            for i in range(3):
                w = p_m[:, i * D:(i + 1) * D]
                w = w.rearrange("p (t h d) -> p h d t", h=2, d=DH) if i == 1 else w.rearrange("p (j s d) -> p s d j", s=S, d=DH)
                to = lambda t, i=i: t[:, i, :].rearrange("p (a b c) -> p a b c", a=2, b=DH)
                nc.vector.tensor_copy(to(w_hi), w).then_inc(w_step, 1)
                dve.wait_ge(w_step, i + 1)
                nc.vector.tensor_tensor(to(w_lo), w, f32(to(w_hi)), ALU.subtract).then_inc(w_split_done, 1)
            nc.vector.tensor_copy(r_both[:, 0], r_raw[:]).then_inc(w_step, 1)
            dve.wait_ge(w_step, 4)
            nc.vector.tensor_tensor(r_both[:, 1], r_raw[:], f32(r_both[:, 0]), ALU.subtract).then_inc(w_split_done, 1)

            def split_weights():
                dve.wait_ge(up_hi_ready, 1)
                hi, lo = (w[:].rearrange("p e h -> p (e h)") for w in (up_hi, up_lo))
                nc.vector.tensor_tensor(lo, raw_weights(), f32(hi), ALU.subtract).then_inc(up_split, 1)
                for i, raw in enumerate(raw_down()):
                    hi, lo = (w[:, 2 * i:2 * i + 2].rearrange("p e c d -> p (e c d)") for w in (dn_hi, dn_lo))
                    dve.wait_ge(dn_hi_ready, i + 1)
                    nc.vector.tensor_tensor(lo, raw, f32(hi), ALU.subtract).then_inc(dn_split, 1)
                dve.wait_ge(up_split, 1)
                dve.wait_ge(dn_split, 4)
                nc.vector.memset(v_rows[:], 0.0).then_inc(v_zeroed, 1)
                dve.wait_ge(v_zeroed, 1)
                for hp in range(2):
                    for r in range(PAIRS):
                        nc.vector.memset(v_rows[SEQ * hp:SEQ * (hp + 1), r, :, hp, DH * T:], 1.0).then_inc(v_zeroed, 1)
                nc.vector.memset(f32(wT[:]), 0.0).then_inc(zeroed, 1)
                dve.wait_ge(pool_const, 8)
                nc.vector.tensor_copy(pick[:].rearrange("p e m -> p (e m)"), raw_pick()).then_inc(pick_ready, 1)
                dve.wait_ge(pick_ready, 1)
                dve.wait_ge(zeroed, 2)

            def moments(g, k, src):
                for r in range(PAIRS):
                    i = nc.vector.bn_stats(stats[:, r, :], src[:, r, :])
                i.then_inc(ln_step[k], 1)
                dve.wait_ge(ln_step[k], 2 * g + 1)
                nc.vector.memset(var_eps[:], 0.0)
                for r in range(PAIRS):
                    i = nc.vector.bn_aggr(mean_var[:, r, :], stats[:, r, :])
                i.then_inc(ln_step[k], 1)
                dve.wait_ge(ln_step[k], 2 * g + 2)
                nc.vector.tensor_scalar(var_eps[:], mean_var[:, :, 1], EPS, None, ALU.add).then_inc(var_ready[k], 1)

            def normalise(g, k, src):
                dve.wait_ge(rstd_ready[k], g + 1)
                for r in range(PAIRS):
                    i = nc.vector.tensor_scalar(xn[:, r, :], src[:, r, :], mean_var[:, r, 0:1], rstd[:, r:r + 1],
                                                ALU.subtract, ALU.mult)
                i.then_inc(xn_ready[k], 1)

            def front(g, odd, slot):
                if slot == NORM1:
                    dve.wait_ge(x_loaded, 16 * (g + 1))
                    moments(g, 0, x_in[:, odd])
                if slot == NORM1 + 1:
                    if begun(g, 2):
                        dve.wait_ge(x2_turned, g - 1)
                    normalise(g, 0, x_in[:, odd])
                if slot == TURN_C:
                    dve.wait_ge(cT_hi_ready, g + 1)
                    nc.vector.tensor_tensor(cT_lo[:], p_t[:], f32(cT_hi[:]), ALU.subtract).then_inc(cT_lo_ready, 1)
                if slot == TURN_X:
                    dve.wait_ge(xT_hi_ready, g + 1)
                    nc.vector.tensor_tensor(xT_lo[:], p_t[:], f32(xT_hi[:]), ALU.subtract).then_inc(xT_lo_ready, 1)
                if slot == k_out(g):
                    dve.wait_ge(k_hi_ready, g + 1)
                    for b in range(2):
                        i = nc.vector.scalar_tensor_tensor(
                            out=k_lo[:, b, :, :], in0=p_t[:].rearrange("p (r b k) -> p b r k", b=2, k=SEQ)[:, b, :, :],
                            scalar=0.0, in1=f32(k_hi[:, b, :, :]), op0=ALU.max, op1=ALU.subtract)
                    i.then_inc(k_lo_ready, 1)
                if slot == Q_OUT:
                    if begun(g):
                        dve.wait_ge(q_placed, q_moves(g))
                    dve.wait_ge(q_made, g + 1)
                    nc.vector.tensor_scalar(q_hi[:].rearrange("p b k r -> p (b k) r"), p_t[:].rearrange("p (r m) -> p m r", r=PAIRS),
                                            0.0, None, ALU.max).then_inc(q_hi_ready, 1)
                    dve.wait_ge(q_hi_ready, g + 1)
                    nc.vector.scalar_tensor_tensor(
                        out=q_lo[:].rearrange("p b k r -> p (b k) r"), in0=p_t[:].rearrange("p (r m) -> p m r", r=PAIRS),
                        scalar=0.0, in1=f32(q_hi[:]).rearrange("p b k r -> p (b k) r"), op0=ALU.max,
                        op1=ALU.subtract).then_inc(q_lo_ready, 1)
                if slot == V_MOVE and not begun(g):
                    split_weights()

            def turned_out(g, r):
                dve.wait_ge(turned, PAIRS * g + r + 1)
                if begun(g):
                    dve.wait_ge(av_done, PAIRS * g + r - 1)
                nc.vector.tensor_copy(probsT[:, r % 2].rearrange("p t m -> p (t m)"),
                                      pair_bank(g, r)[:].rearrange("p s m -> p (s m)")).then_inc(pT_ready, 1)

            def divide(g, r):
                dve.wait_ge(av_done, PAIRS * g + r + 1)
                o = p_m[:, 0:T * 4 * (DH + 1)].rearrange("p (t b h d) -> p b t h d", t=T, b=2, h=2)
                inv = inv_sum[:].rearrange("p (t h) -> p t h", h=2)
                for b in range(2):
                    rows = slice(SEQ * b, SEQ * (b + 1))
                    i = nc.vector.reciprocal(inv[rows], o[rows, b, :, :, DH])
                i.then_inc(sums_ready, 1)
                dve.wait_ge(sums_ready, PAIRS * g + r + 1)
                if r >= 2:
                    dve.wait_ge(x1_ready, PAIRS * g + r - 1)
                for b in range(2):
                    rows = slice(SEQ * b, SEQ * (b + 1))
                    i = nc.vector.tensor_tensor(att[rows, r % 2].rearrange("p (t h) d -> p t h d", h=2), o[rows, b, :, :, 0:DH],
                                                inv[rows].unsqueeze(3).broadcast_to([SEQ, T, 2, DH]), ALU.mult)
                i.then_inc(o_read, 1)

            def back(g, odd, slot, beside):
                if slot < EXP and slot % SCORE_EVERY < 2:
                    r = slot // SCORE_EVERY
                    sc = pair_bank(g, r)[:].rearrange("p s (j k) -> p (s j) k", k=SEQ)
                    if slot % SCORE_EVERY == 0:
                        dve.wait_ge(scores_ready, PAIRS * g + r + 1)
                        nc.vector.tensor_reduce(row_max[:, r % 2], sc, AX.X, ALU.max).then_inc(max_ready, 1)
                    else:
                        dve.wait_ge(max_ready, PAIRS * g + r + 1)
                        nc.vector.tensor_tensor(probs[:, r, :, :], sc, row_max[:, r % 2].unsqueeze(2).broadcast_to([P, HEADS, SEQ]),
                                                ALU.subtract).then_inc(shifted, 1)
                if slot == EXP:
                    turned_out(g, 0)
                    turned_out(g, 1)
                    divide(g, 0)
                if EXP + 2 < slot < EXP + 2 + PAIRS:
                    divide(g, slot - EXP - 2)
                if slot == NORM2:
                    dve.wait_ge(x1_ready, PAIRS * (g + 1))
                    moments(g, 1, x1[:, odd])
                if slot == NORM2 + 1:
                    dve.wait_ge(x_turned, g + 1 + beside)
                    normalise(g, 1, x1[:, odd])
                if slot == TURN_X2:
                    dve.wait_ge(x2_hi_ready, g + 1)
                    nc.vector.tensor_tensor(x2_lo[:, odd, :], p_t[:], f32(x2_hi[:, odd, :]), ALU.subtract).then_inc(x2_lo_ready, 1)
                if slot == ROUTE + 1:
                    dve.wait_ge(logits_ready, g + 1)
                    lg = p_m[:, 0:PAIRS * 2 * E].rearrange("p (r a e) -> p a r e", a=2, e=E)
                    nc.vector.tensor_copy(logits_low[:], lg[:, 1]).then_inc(logits_summed, 1)
                    dve.wait_ge(logits_summed, 2 * g + 1)
                    nc.vector.tensor_tensor(logits[:], lg[:, 0], logits_low[:], ALU.add).then_inc(logits_summed, 1)
                    dve.wait_ge(logits_summed, 2 * g + 2)
                    nc.vector.tensor_reduce(logit_max[:], logits[:], AX.X, ALU.max).then_inc(route_step, 1)
                    dve.wait_ge(route_step, 6 * g + 1)
                    nc.vector.tensor_tensor(logits[:], logits[:], logit_max[:].unsqueeze(2).broadcast_to([P, PAIRS, E]),
                                            ALU.subtract).then_inc(logits_read, 1)
                if slot == ROUTE + 2:
                    dve.wait_ge(logits_read, g + 1)
                    other = logits[:].unsqueeze(2).broadcast_to([P, PAIRS, E, E])
                    own = logits[:].unsqueeze(3).broadcast_to([P, PAIRS, E, E])
                    nc.vector.tensor_tensor(above, other, own, ALU.is_gt)
                    nc.vector.tensor_tensor(same, other, own, ALU.is_equal).then_inc(compared, 1)
                if slot == ROUTE + 4:
                    dve.wait_ge(compared, g + 1)
                    nc.vector.tensor_tensor(same, same, earlier[:].unsqueeze(1).broadcast_to([P, PAIRS, E, E]),
                                            ALU.mult).then_inc(ties_marked, 1)
                    dve.wait_ge(ties_marked, g + 1)
                    nc.vector.tensor_tensor(above, above, same, ALU.add).then_inc(rank_in, 1)
                if slot == ROUTE + 5:
                    dve.wait_ge(rank_in, g + 1)
                    nc.vector.tensor_reduce(rank[:], above, AX.X, ALU.add).then_inc(route_step, 1)
                if slot == ROUTE + 7:
                    dve.wait_ge(powers, PAIRS * (g + 1))
                    dve.wait_ge(route_step, 6 * g + 2)
                    nc.vector.scalar_tensor_tensor(out=w_sel[:].rearrange("p r e -> p (r e)"), in0=rank[:].rearrange("p r e -> p (r e)"),
                                                   scalar=TOPK - 0.5, in1=expert_p[:].rearrange("p r e -> p (r e)"),
                                                   op0=ALU.is_lt, op1=ALU.mult).then_inc(route_step, 1)
                    dve.wait_ge(route_step, 6 * g + 3)
                    nc.vector.tensor_reduce(w_sum[:], w_sel[:], AX.X, ALU.add).then_inc(route_step, 1)
                    dve.wait_ge(route_step, 6 * g + 4)
                    nc.vector.reciprocal(w_inv[:], w_sum[:]).then_inc(route_step, 1)
                    dve.wait_ge(route_step, 6 * g + 5)
                    nc.vector.tensor_tensor(w_norm[:], w_sel[:], w_inv[:].unsqueeze(2).broadcast_to([P, PAIRS, E]),
                                            ALU.mult).then_inc(route_step, 1)
                    dve.wait_ge(route_step, 6 * g + 6)
                    nc.vector.tensor_copy(w_round[:], w_norm[:]).then_inc(round_done, 1)
                    dve.wait_ge(round_done, g + 1)
                    nc.vector.tensor_copy(w_split[:, :, 0, :], f32(w_round[:]))
                    nc.vector.tensor_tensor(w_split[:, :, 1, :], w_norm[:], f32(w_round[:]), ALU.subtract).then_inc(weights_ready, 1)

            def weigh(g, e):
                dve.wait_ge(down_done, U * g + CH * (e + 1))
                dve.wait_ge(wb_ready, E * g + e + 1)
                if e >= 2:
                    dve.wait_ge(acc_ready, (E - 1) * g + max(e - 2, 1))
                elif begun(g):
                    dve.wait_ge(acc_ready, (E - 1) * g)
                nc.vector.tensor_tensor(prod[:, e % 2, :], p_y[:, e % 2, :], wb[:], ALU.mult).then_inc(prod_ready, 1)

            def residual(g, odd):
                dve.wait_ge(out_turned, g + 1)
                if begun(g):
                    dve.wait_ge(stored, 16 * g)
                nc.vector.tensor_tensor(o_sb[:].rearrange("p r d -> p (r d)"), p_m[:],
                                        x1[:, odd].rearrange("p r d -> p (r d)"), ALU.add).then_inc(out_ready, 1)

            def experts(g, odd, slot):
                first = not begun(g)
                if slot % CH == 3:
                    if slot > CH:
                        weigh(g, slot // CH - 1)
                    elif not first:
                        weigh(g - 1, E - 1)
                dve.wait_ge(h_full_ready, U * g + slot + 1)
                if slot in DVE_HI:
                    if slot >= NH or not first:
                        dve.wait_ge(down_done, U * g + slot - NH + 1)
                    nc.vector.tensor_copy(h_hi[:, slot % NH, :], h_full[:, slot % NH, :]).then_inc(h_hi_dve, 1)
                if slot in DVE_LOW:
                    high_done(dve, g, slot)
                    nc.vector.tensor_tensor(h_lo[:, slot % NH, :], h_full[:, slot % NH, :], f32(h_hi[:, slot % NH, :]),
                                            ALU.subtract).then_inc(h_lo_dve, 1)
                if slot == OUT and not first:
                    residual(g - 1, 1 - odd)

            def drain(g):
                weigh(g - 1, E - 1)
                residual(g - 1, 1)

            by_group(dve, front, back, experts, drain)

        @block.tensor
        def _(pe):
            pe.wait_ge(w_loaded, 64)
            pe.wait_ge(pool_const, 5)
            for i in range(3):
                mm = nc.tensor.transpose(p_m[:, i * D:(i + 1) * D], w_raw[:, i, :], ident[:])
            mm.then_inc(w_turned, 1)
            pe.wait_ge(w_split_done, 4)

            def three(out, lhs_hi, lhs_lo, rhs_hi, rhs_lo, start=True, stop=True):
                nc.tensor.matmul(out, lhs_hi, rhs_hi, start=start, stop=False)
                nc.tensor.matmul(out, lhs_hi, rhs_lo, start=False, stop=False)
                return nc.tensor.matmul(out, lhs_lo, rhs_hi, start=False, stop=stop)

            def turn(bank, src):
                for r in range(PAIRS):
                    mm = nc.tensor.transpose(bank[:, r * P:(r + 1) * P], src[:, r, :], ident[:])
                return mm

            def front(g, odd, slot):
                if slot == TURN_C:
                    pe.wait_ge(c_loaded, 16 * (g + 1))
                    if begun(g):
                        pe.wait_ge(v_ready, g)
                    if begun(g, 2):
                        pe.wait_ge(x2_hi_ready, g - 1)
                        pe.wait_ge(x2_lo_ready, g - 1)
                    turn(p_t, c_in).then_inc(c_turned, 1)
                if slot == TURN_X:
                    pe.wait_ge(xn_ready[0], g + 1)
                    if begun(g):
                        pe.wait_ge(cT_hi_ready, g + 1)
                        pe.wait_ge(cT_lo_ready, g + 1)
                    else:
                        pe.wait_ge(k_hi_ready, 1)
                        pe.wait_ge(k_lo_ready, 1)
                    turn(p_t, xn).then_inc(x_turned, 1)
                if slot == k_out(g):
                    if begun(g):
                        pe.wait_ge(xT_hi_ready, g + 1)
                        pe.wait_ge(xT_lo_ready, g + 1)
                    pe.wait_ge(cT_hi_ready, g + 1)
                    pe.wait_ge(cT_lo_ready, g + 1)
                    three(p_t[:], w_hi[:, 0, :], w_lo[:, 0, :], cT_hi[:], cT_lo[:]).then_inc(k_made, 1)
                if slot == Q_OUT:
                    pe.wait_ge(k_hi_ready, g + 1)
                    pe.wait_ge(k_lo_ready, g + 1)
                    pe.wait_ge(xT_hi_ready, g + 1)
                    pe.wait_ge(xT_lo_ready, g + 1)
                    three(p_t[:], w_hi[:, 2, :], w_lo[:, 2, :], xT_hi[:], xT_lo[:]).then_inc(q_made, 1)
                if slot == V_OUT:
                    pe.wait_ge(q_hi_ready, g + 1)
                    pe.wait_ge(q_lo_ready, g + 1)
                    for r in range(PAIRS):
                        tok = slice(r * P, (r + 1) * P)
                        mm = three(p_t[:, tok], cT_hi[:, tok], cT_lo[:, tok], w_hi[:, 1, :], w_lo[:, 1, :])
                    mm.then_inc(v_made, 1)

            def back(g, odd, slot, beside):
                if slot < EXP and slot % SCORE_EVERY == 0:
                    r = slot // SCORE_EVERY
                    if r == 0:
                        if begun(g):
                            pe.wait_ge(pT_ready, PAIRS * g)
                        pe.wait_ge(k_placed, S * SPREAD * (g + 1))
                        pe.wait_ge(q_placed, q_moves(g + 1))
                        if not begun(g):
                            pe.wait_ge(q_placed_by_pool, SPREAD)
                    elif begun(g):
                        pe.wait_ge(shifted, PAIRS * g + r)
                    elif r > 1:
                        pe.wait_ge(shifted, r - 1)
                    for j in range(J):
                        mm = nc.tensor.matmul(pair_bank(g, r)[:, j // 4, j % 4 * S * SEQ:(j % 4 + 1) * S * SEQ], q_rows[:, j, :, r],
                                              k_rows[:, j, :, r, :], start=True, stop=True)
                    mm.then_inc(scores_ready, 1)
                if EXP + 1 <= slot < EXP + 1 + PAIRS:
                    r = slot - EXP - 1
                    if r == 0:
                        pe.wait_ge(shifted, PAIRS * (g + 1))
                    elif begun(g):
                        pe.wait_ge(pT_ready, PAIRS * g + r)
                    elif r > 1:
                        pe.wait_ge(pT_ready, r - 1)
                    pe.wait_ge(exp_done, PAIRS * g + r + 1)
                    for t in range(T):
                        mm = nc.tensor.transpose(pair_bank(g, r)[:, t // 4, t % 4 * P:(t % 4 + 1) * P],
                                                 probs[:, r, 2 * t:2 * t + 2, :].rearrange("p h k -> p (h k)"), ident[:])
                    mm.then_inc(turned, 1)
                if EXP + 2 <= slot < EXP + 2 + PAIRS:
                    r = slot - EXP - 2
                    pe.wait_ge(pT_ready, PAIRS * g + r + 1)
                    if r == 0:
                        pe.wait_ge(v_placed, 16 * 4 * (g + 1))
                        if begun(g, 2):
                            pe.wait_ge(out_ready, g - 1)
                    else:
                        pe.wait_ge(o_read, PAIRS * g + r)
                    vr = v_rows[:, r, :, :, :].rearrange("p b h (d t) -> p (b h) d t", t=T)
                    w = 4 * (DH + 1)
                    for t in range(T):
                        mm = nc.tensor.matmul(p_m[:, t * w:(t + 1) * w], probsT[:, r % 2, t, :], vr[:, :, :, t], start=True, stop=True)
                    mm.then_inc(av_done, 1)
                if slot == TURN_X2:
                    pe.wait_ge(xn_ready[1], g + 1)
                    if beside:
                        pe.wait_ge(v_ready, g + 2)
                    turn(p_t, xn).then_inc(x2_turned, 1)
                if slot == ROUTE:
                    pe.wait_ge(x2_hi_ready, g + 1)
                    pe.wait_ge(x2_lo_ready, g + 1)
                    pe.wait_ge(o_read, PAIRS * (g + 1))
                    for r in range(PAIRS):
                        tok = slice(r * P, (r + 1) * P)
                        nc.tensor.matmul(p_m[:, 2 * r * E:2 * (r + 1) * E], x2_hi[:, odd, tok], r_both[:].rearrange("p a e -> p (a e)"),
                                         start=True, stop=False)
                        mm = nc.tensor.matmul(p_m[:, 2 * r * E:(2 * r + 1) * E], x2_lo[:, odd, tok], r_both[:, 0], start=False, stop=True)
                    mm.then_inc(logits_ready, 1)

            def down(g, unit):
                e, c = unit // CH, unit % CH
                high_done(pe, g, unit)
                low_done(pe, g, unit)
                if c == 0 and (e or begun(g)):
                    pe.wait_ge(wb_ready, E * g + e)
                three(p_y[:, e % 2, :], dn_hi[:, e, c, :], dn_lo[:, e, c, :], h_hi[:, unit % NH, :], h_lo[:, unit % NH, :],
                      start=(c == 0), stop=(c == CH - 1)).then_inc(down_done, 1)

            def turn_out(g):
                pe.wait_ge(acc_ready, (E - 1) * (g + 1))
                turn(p_m, acc[:].rearrange("p (r m) -> p r m", r=PAIRS)).then_inc(out_turned, 1)

            def spread_weight(g, e):
                if e == 0:
                    pe.wait_ge(wT_ready, g + 1)
                if e or begun(g):
                    pe.wait_ge(prod_ready, E * g + e)
                nc.tensor.matmul(p_y[:, (e + 1) % 2, :], pick[:, e, :], wT[:], start=True, stop=True).then_inc(wb_made, 1)

            def experts(g, odd, slot):
                first = not begun(g)
                e, c = slot // CH, slot % CH
                if slot == 0:
                    pe.wait_ge(x2_lo_ready, g + 1)
                    pe.wait_ge(x2_hi_ready, g + 1)
                    if first:
                        pe.wait_ge(dn_split, 4)
                if slot >= 2 or not first:
                    if (slot - 2) % U in ACT_HI:
                        high_done(pe, g, slot - 2)
                    else:
                        pe.wait_ge(h_full_ready, U * g + slot - 1)
                hid = slice(c * P, (c + 1) * P)
                three(p_u[:, slot % 2, :], up_hi[:, e, hid], up_lo[:, e, hid], x2_hi[:, odd, :], x2_lo[:, odd, :]).then_inc(up_done, 1)
                if slot >= LAG:
                    down(g, slot - LAG)
                elif not first:
                    down(g - 1, U + slot - LAG)
                if c == 1:
                    if e:
                        spread_weight(g, e - 1)
                    elif not first:
                        spread_weight(g - 1, E - 1)
                if slot == W_TURN:
                    pe.wait_ge(weights_ready, g + 1)
                    for r in range(PAIRS):
                        mm = nc.tensor.transpose(p_m[0:2 * E, r * P:(r + 1) * P],
                                                 w_split[:, r, :, :].rearrange("p a e -> p (a e)"), ident[:])
                    mm.then_inc(wT_turned, 1)
                if slot == OUT and not first:
                    turn_out(g - 1)

            def drain(g):
                for unit in range(U - LAG, U):
                    down(g - 1, unit)
                    if unit == U - 2:
                        spread_weight(g - 1, E - 1)
                turn_out(g - 1)

            by_group(pe, front, back, experts, drain)


_INS = ['x', 'ctx_1024', 'L0_xattn_Wq', 'L0_xattn_Wk', 'L0_xattn_Wv', 'L0_ffn_router_w', 'L0_ffn_up_w', 'L0_ffn_down_w']
_OUTS = [((128, 64, 128), 'float32')]


def kernel(**inputs):
    import numpy as _np
    import concourse.bacc as _bacc
    from concourse import mybir as _mybir
    from concourse.bass_utils import run_bass_kernel_spmd as _run

    nc = _bacc.Bacc("TRN2", target_bir_lowering=False, num_devices=1)
    arrays, args = {}, []
    for name in _INS:
        a = _np.ascontiguousarray(inputs[name])
        arrays[f"in_{name}_dram"] = a
        args.append(nc.dram_tensor(f"in_{name}_dram", a.shape, _mybir.dt.from_np(a.dtype), kind="ExternalInput").ap())
    for i, (shape, dtype) in enumerate(_OUTS):
        dt = _mybir.dt.from_np(_np.dtype(dtype))
        args.append(nc.dram_tensor(f"out_{i}_dram", shape, dt, kind="ExternalOutput").ap())
    build(nc, *args)
    r = _run(nc, [arrays], core_ids=[0])
    return r.results[0]["out_0_dram"]
```
